# Optimizing a Trainium2 kernel written in Bass

```python
import numpy as np
import jax
import jax.numpy as jnp

def _softmax(x, axis=-1):
    return jax.nn.softmax(x, axis=axis)

def _gelu(x):
    return jax.nn.gelu(x, approximate=True)

def _silu(x):
    return jax.nn.silu(x)

def _sigmoid(x):
    return jax.nn.sigmoid(x)

def _layernorm(x, axis=-1, eps=1e-05):
    m = jnp.mean(x, axis=axis, keepdims=True)
    v = jnp.var(x, axis=axis, keepdims=True)
    return (x - m) / jnp.sqrt(v + eps)

def _scatter_add(tgt, idx, src, axis=0):
    return tgt.at[idx].add(src)

def _segment_sum(src, seg, n):
    return jax.ops.segment_sum(src, seg, n)
kernel_name = 'mk_conv_preact_d2_conv_nchw1024_r2_9e8e17'

def setup_inputs(seed: int=0):
    np.random.seed(seed)
    _w = jnp.asarray

    def _rec_inputs():
        import jax
        import jax.numpy as jnp
        _gk = jax.random.key(seed)
        x = -0.0003929 + 0.9999 * jax.random.normal(jax.random.fold_in(_gk, 1), (16, 512, 32, 32), jnp.float32)
        return x
    x = _rec_inputs()

    def _L0_conv_setup():
        import jax, jax.numpy as jnp
        import numpy as np
        from jax import lax
        GROUPS = 8
        K = 3
        STRIDE = 1
        PAD = 1
        key = jax.random.key(seed)
        k1, k2, k3 = jax.random.split(key, 3)
        B, Cin, H, Wd = (16, 512, 32, 32)
        gin = Cin // GROUPS
        gout = 512 // GROUPS
        x = jax.random.normal(k1, (B, Cin, H, Wd), dtype=jnp.float32)
        W = jax.random.normal(k2, (GROUPS, gout, gin * K * K), dtype=jnp.float32) * 0.02
        b = jax.random.normal(k3, (GROUPS, gout), dtype=jnp.float32) * 0.02
        return {'x': x, 'W': W, 'b': b}
    _L0_conv_all = _L0_conv_setup()
    _L0_conv_in = {k: v for k, v in _L0_conv_all.items() if k in ('W', 'b')}
    del _L0_conv_all

    def _L1_conv_setup():
        import jax, jax.numpy as jnp
        import numpy as np
        EPS = 1e-05

        def _bn(x, g, b, m, v):
            s = (g / jnp.sqrt(v + EPS))[None, :, None, None]
            return (x - m[None, :, None, None]) * s + b[None, :, None, None]

        def _conv1x1(x, w, b):
            return jnp.einsum('bihw,oi->bohw', x, w) + b[None, :, None, None]

        def _conv3x3(x, w, b):
            y = jax.lax.conv_general_dilated(x, w, (1, 1), ((1, 1), (1, 1)), dimension_numbers=('NCHW', 'OIHW', 'NCHW'))
            return y + b[None, :, None, None]

        def _deform_conv3x3(x, offset, w, b):
            B, C, H, W = x.shape
            off = offset.reshape(B, 9, 2, H, W)
            dy, dx = (off[:, :, 0], off[:, :, 1])
            k = jnp.arange(9)
            ky = (k // 3 - 1).astype(x.dtype)
            kx = (k % 3 - 1).astype(x.dtype)
            hh = jnp.arange(H, dtype=x.dtype)
            ww = jnp.arange(W, dtype=x.dtype)
            py = hh[None, None, :, None] + ky[None, :, None, None] + dy
            px = ww[None, None, None, :] + kx[None, :, None, None] + dx
            y0 = jnp.floor(py)
            x0 = jnp.floor(px)
            ly = py - y0
            lx = px - x0
            y0i = y0.astype(jnp.int32)
            x0i = x0.astype(jnp.int32)
            xf = x.reshape(B, C, H * W)

            def gather(yi, xi):
                valid = (yi >= 0) & (yi < H) & (xi >= 0) & (xi < W)
                idx = jnp.clip(yi, 0, H - 1) * W + jnp.clip(xi, 0, W - 1)
                idx = idx.reshape(B, 1, -1)
                g = jnp.take_along_axis(xf, jnp.broadcast_to(idx, (B, C, idx.shape[-1])), axis=2)
                return g.reshape(B, C, 9, H, W) * valid[:, None].astype(x.dtype)
            v00 = gather(y0i, x0i)
            v01 = gather(y0i, x0i + 1)
            v10 = gather(y0i + 1, x0i)
            v11 = gather(y0i + 1, x0i + 1)
            wy1 = ly[:, None]
            wy0 = 1.0 - wy1
            wx1 = lx[:, None]
            wx0 = 1.0 - wx1
            val = v00 * wy0 * wx0 + v01 * wy0 * wx1 + v10 * wy1 * wx0 + v11 * wy1 * wx1
            Co = w.shape[0]
            return jnp.einsum('bckhw,ock->bohw', val, w.reshape(Co, C, 9)) + b[None, :, None, None]
        key = jax.random.key(seed)
        ks = jax.random.split(key, 24)
        B, Cin, H, W = (16, 512, 32, 32)
        C = 128
        f = jnp.float32
        d = {}
        d['x'] = jax.random.normal(ks[0], (B, Cin, H, W), f)
        d['conv1_w'] = jax.random.normal(ks[1], (C, Cin), f) * (1.0 / np.sqrt(Cin))
        d['conv1_b'] = jax.random.normal(ks[2], (C,), f) * 0.05
        d['bn1_g'] = jax.random.uniform(ks[3], (C,), f, 0.5, 1.5)
        d['bn1_b'] = jax.random.normal(ks[4], (C,), f) * 0.05
        d['bn1_m'] = jax.random.normal(ks[5], (C,), f) * 0.05
        d['bn1_v'] = jax.random.uniform(ks[6], (C,), f, 0.5, 1.5)
        d['off_w'] = jax.random.normal(ks[7], (18, C, 3, 3), f) * 0.01
        d['off_b'] = jax.random.normal(ks[8], (18,), f) * 0.01
        d['dconv_w'] = jax.random.normal(ks[9], (C, C, 3, 3), f) * (1.0 / np.sqrt(9 * C))
        d['dconv_b'] = jax.random.normal(ks[10], (C,), f) * 0.05
        d['bn2_g'] = jax.random.uniform(ks[11], (C,), f, 0.5, 1.5)
        d['bn2_b'] = jax.random.normal(ks[12], (C,), f) * 0.05
        d['bn2_m'] = jax.random.normal(ks[13], (C,), f) * 0.05
        d['bn2_v'] = jax.random.uniform(ks[14], (C,), f, 0.5, 1.5)
        d['conv2_w'] = jax.random.normal(ks[15], (4 * C, C), f) * (1.0 / np.sqrt(C))
        d['conv2_b'] = jax.random.normal(ks[16], (4 * C,), f) * 0.05
        d['bn3_g'] = jax.random.uniform(ks[17], (4 * C,), f, 0.5, 1.5)
        d['bn3_b'] = jax.random.normal(ks[18], (4 * C,), f) * 0.05
        d['bn3_m'] = jax.random.normal(ks[19], (4 * C,), f) * 0.05
        d['bn3_v'] = jax.random.uniform(ks[20], (4 * C,), f, 0.5, 1.5)
        return d
    _L1_conv_all = _L1_conv_setup()
    _L1_conv_in = {k: v for k, v in _L1_conv_all.items() if k in ('conv1_w', 'conv1_b', 'bn1_g', 'bn1_b', 'bn1_m', 'bn1_v', 'off_w', 'off_b', 'dconv_w', 'dconv_b', 'bn2_g', 'bn2_b', 'bn2_m', 'bn2_v', 'conv2_w', 'conv2_b', 'bn3_g', 'bn3_b', 'bn3_m', 'bn3_v')}
    del _L1_conv_all
    return {'x': x, 'L0_conv_W': _L0_conv_in['W'], 'L0_conv_b': _L0_conv_in['b'], 'L1_conv_conv1_w': _L1_conv_in['conv1_w'], 'L1_conv_conv1_b': _L1_conv_in['conv1_b'], 'L1_conv_bn1_g': _L1_conv_in['bn1_g'], 'L1_conv_bn1_b': _L1_conv_in['bn1_b'], 'L1_conv_bn1_m': _L1_conv_in['bn1_m'], 'L1_conv_bn1_v': _L1_conv_in['bn1_v'], 'L1_conv_off_w': _L1_conv_in['off_w'], 'L1_conv_off_b': _L1_conv_in['off_b'], 'L1_conv_dconv_w': _L1_conv_in['dconv_w'], 'L1_conv_dconv_b': _L1_conv_in['dconv_b'], 'L1_conv_bn2_g': _L1_conv_in['bn2_g'], 'L1_conv_bn2_b': _L1_conv_in['bn2_b'], 'L1_conv_bn2_m': _L1_conv_in['bn2_m'], 'L1_conv_bn2_v': _L1_conv_in['bn2_v'], 'L1_conv_conv2_w': _L1_conv_in['conv2_w'], 'L1_conv_conv2_b': _L1_conv_in['conv2_b'], 'L1_conv_bn3_g': _L1_conv_in['bn3_g'], 'L1_conv_bn3_b': _L1_conv_in['bn3_b'], 'L1_conv_bn3_m': _L1_conv_in['bn3_m'], 'L1_conv_bn3_v': _L1_conv_in['bn3_v']}

def reference(x, L0_conv_W, L0_conv_b, L1_conv_conv1_w, L1_conv_conv1_b, L1_conv_bn1_g, L1_conv_bn1_b, L1_conv_bn1_m, L1_conv_bn1_v, L1_conv_off_w, L1_conv_off_b, L1_conv_dconv_w, L1_conv_dconv_b, L1_conv_bn2_g, L1_conv_bn2_b, L1_conv_bn2_m, L1_conv_bn2_v, L1_conv_conv2_w, L1_conv_conv2_b, L1_conv_bn3_g, L1_conv_bn3_b, L1_conv_bn3_m, L1_conv_bn3_v):
    import jax
    import jax.numpy as jnp

    def _L0_conv_ref(x, W, b):
        import jax, jax.numpy as jnp
        import numpy as np
        from jax import lax
        GROUPS = 8
        K = 3
        STRIDE = 1
        PAD = 1
        B, Cin, H, Wd = x.shape
        G, gout, _ = W.shape
        gin = Cin // G
        kernel = W.reshape(G * gout, gin, K, K)
        out = lax.conv_general_dilated(x, kernel, window_strides=(STRIDE, STRIDE), padding=[(PAD, PAD), (PAD, PAD)], dimension_numbers=('NCHW', 'OIHW', 'NCHW'), feature_group_count=G)
        out = out + b.reshape(-1)[None, :, None, None]
        Ho = (H + 2 * PAD - K) // STRIDE + 1
        Wo = (Wd + 2 * PAD - K) // STRIDE + 1
        L = Ho * Wo
        out = out.reshape(B, G, gout, L).transpose(0, 1, 3, 2)
        out = out.reshape(B, G * gout, Ho, Wo)
        return out

    def _L1_conv_ref(x, conv1_w, conv1_b, bn1_g, bn1_b, bn1_m, bn1_v, off_w, off_b, dconv_w, dconv_b, bn2_g, bn2_b, bn2_m, bn2_v, conv2_w, conv2_b, bn3_g, bn3_b, bn3_m, bn3_v):
        import jax, jax.numpy as jnp
        import numpy as np
        EPS = 1e-05

        def _bn(x, g, b, m, v):
            s = (g / jnp.sqrt(v + EPS))[None, :, None, None]
            return (x - m[None, :, None, None]) * s + b[None, :, None, None]

        def _conv1x1(x, w, b):
            return jnp.einsum('bihw,oi->bohw', x, w) + b[None, :, None, None]

        def _conv3x3(x, w, b):
            y = jax.lax.conv_general_dilated(x, w, (1, 1), ((1, 1), (1, 1)), dimension_numbers=('NCHW', 'OIHW', 'NCHW'))
            return y + b[None, :, None, None]

        def _deform_conv3x3(x, offset, w, b):
            B, C, H, W = x.shape
            off = offset.reshape(B, 9, 2, H, W)
            dy, dx = (off[:, :, 0], off[:, :, 1])
            k = jnp.arange(9)
            ky = (k // 3 - 1).astype(x.dtype)
            kx = (k % 3 - 1).astype(x.dtype)
            hh = jnp.arange(H, dtype=x.dtype)
            ww = jnp.arange(W, dtype=x.dtype)
            py = hh[None, None, :, None] + ky[None, :, None, None] + dy
            px = ww[None, None, None, :] + kx[None, :, None, None] + dx
            y0 = jnp.floor(py)
            x0 = jnp.floor(px)
            ly = py - y0
            lx = px - x0
            y0i = y0.astype(jnp.int32)
            x0i = x0.astype(jnp.int32)
            xf = x.reshape(B, C, H * W)

            def gather(yi, xi):
                valid = (yi >= 0) & (yi < H) & (xi >= 0) & (xi < W)
                idx = jnp.clip(yi, 0, H - 1) * W + jnp.clip(xi, 0, W - 1)
                idx = idx.reshape(B, 1, -1)
                g = jnp.take_along_axis(xf, jnp.broadcast_to(idx, (B, C, idx.shape[-1])), axis=2)
                return g.reshape(B, C, 9, H, W) * valid[:, None].astype(x.dtype)
            v00 = gather(y0i, x0i)
            v01 = gather(y0i, x0i + 1)
            v10 = gather(y0i + 1, x0i)
            v11 = gather(y0i + 1, x0i + 1)
            wy1 = ly[:, None]
            wy0 = 1.0 - wy1
            wx1 = lx[:, None]
            wx0 = 1.0 - wx1
            val = v00 * wy0 * wx0 + v01 * wy0 * wx1 + v10 * wy1 * wx0 + v11 * wy1 * wx1
            Co = w.shape[0]
            return jnp.einsum('bckhw,ock->bohw', val, w.reshape(Co, C, 9)) + b[None, :, None, None]
        out = jax.nn.relu(_bn(_conv1x1(x, conv1_w, conv1_b), bn1_g, bn1_b, bn1_m, bn1_v))
        offset = _conv3x3(out, off_w, off_b)
        out = _deform_conv3x3(out, offset, dconv_w, dconv_b)
        out = _bn(out, bn2_g, bn2_b, bn2_m, bn2_v)
        out = _conv1x1(out, conv2_w, conv2_b)
        out = jax.nn.relu(_bn(out, bn3_g, bn3_b, bn3_m, bn3_v))
        return out

    def _gn(v, G=32, eps=1e-05):
        B_, C_, H_, W_ = v.shape
        g = v.reshape(B_, G, C_ // G, H_, W_)
        m = jnp.mean(g, axis=(2, 3, 4), keepdims=True)
        s = jnp.var(g, axis=(2, 3, 4), keepdims=True)
        return ((g - m) / jnp.sqrt(s + eps)).reshape(v.shape)

    def _ln_c(v, eps=1e-06):
        m = jnp.mean(v, axis=1, keepdims=True)
        s = jnp.var(v, axis=1, keepdims=True)
        return (v - m) / jnp.sqrt(s + eps)

    def _ln_t(v, eps=1e-05):
        m = jnp.mean(v, axis=-1, keepdims=True)
        s = jnp.var(v, axis=-1, keepdims=True)
        return (v - m) / jnp.sqrt(s + eps)

    def _to_tokens(v):
        B_, C_, H_, W_ = v.shape
        return v.reshape(B_, C_, H_ * W_).transpose(0, 2, 1)

    def _from_tokens(t, like):
        B_, C_, H_, W_ = like.shape
        return t.transpose(0, 2, 1).reshape(B_, C_, H_, W_)
    x = x + _L0_conv_ref(_gn(x), L0_conv_W, L0_conv_b)
    x = x + _L1_conv_ref(_gn(x), L1_conv_conv1_w, L1_conv_conv1_b, L1_conv_bn1_g, L1_conv_bn1_b, L1_conv_bn1_m, L1_conv_bn1_v, L1_conv_off_w, L1_conv_off_b, L1_conv_dconv_w, L1_conv_dconv_b, L1_conv_bn2_g, L1_conv_bn2_b, L1_conv_bn2_m, L1_conv_bn2_v, L1_conv_conv2_w, L1_conv_conv2_b, L1_conv_bn3_g, L1_conv_bn3_b, L1_conv_bn3_m, L1_conv_bn3_v)
    return x

_drawn_inputs = setup_inputs


def setup_inputs(seed=0):
    import zlib

    import numpy as np

    out = dict(_drawn_inputs(seed))
    spreads = {}
    factors = {'L0_conv_b': 3.177, 'L1_conv_off_b': 7.272}
    for name, (base, spread) in spreads.items():
        noise = np.random.default_rng([zlib.crc32(name.encode()), seed]).standard_normal(out[name].shape)
        drawn = base * np.exp(spread * noise) if base else spread * noise
        out[name] = jnp.asarray(drawn.astype(out[name].dtype))
    for name, factor in factors.items():
        out[name] = (out[name] * factor).astype(out[name].dtype)
    return out
```

```python
import concourse.bass as bass
from concourse import mybir
from contextlib import ExitStack


def build_program(nc, x, w_group, b_group, w_in, w_off, b_off, w_def, w_out, bn, eye, fold, blocks, offset_fold,
                  grid, tables, out):
    f32, f16, i32, u32 = mybir.dt.float32, mybir.dt.float16, mybir.dt.int32, mybir.dt.uint32
    ALU = mybir.AluOpType
    ACT = mybir.ActivationFunctionType

    IMAGES, CHANNELS, HEIGHT, WIDTH = 16, 512, 32, 32
    PIX = HEIGHT * WIDTH
    HALF = PIX // 2
    HROWS = HEIGHT // 2
    QUADS = CHANNELS // 128
    GROUPS = 8
    GIN = CHANNELS // GROUPS
    TAPS = 9
    PITCH = WIDTH + 2
    PLANE = PITCH * (HEIGHT + 2)
    TILES = 9
    ROWS = TILES * 128
    HPLANE = PITCH * (HEIGHT + 3)
    NDX = ROWS + PITCH
    CH = 128
    OFFS = 2 * TAPS
    CHUNKS = 2 * TAPS
    RING = 3
    PER = 4
    ROW = 4 * CH
    COLS = PIX // GIN
    EPS = 1e-5

    ctx = ExitStack()
    with ctx:
        def sb(name, shape, dt):
            return ctx.enter_context(nc.sbuf_tensor("sb_" + name, shape, dt))

        def sem(name):
            return ctx.enter_context(nc.semaphore(name))

        x_in = sb("x_in", [128, 2, QUADS, PIX], f32)
        x_mid = sb("x_mid", [128, 2, QUADS, PIX], f32)
        split1 = sb("split1", [128, GROUPS, PLANE], f16)
        wg = sb("wg", [128, GROUPS, TAPS, 2 * GIN], f16)
        conv_sb = sb("conv_sb", [128, 3, PIX], f32)
        norm1 = sb("norm1", [128, PIX], f32)
        norm2 = sb("norm2", [128, PIX], f32)
        split2 = sb("split2", [128, 2, QUADS, PIX], f16)
        h_sb = sb("h_sb", [128, HPLANE], f32)
        h_split = sb("h_split", [128, 2, HPLANE], f16)
        table_sb = sb("table_sb", [128, 2, ROW], f32)
        rows = sb("rows", [128, RING * PER, ROW], f32)
        val = sb("val", [128, 2, PER * CH], f32)
        val_split = sb("val_split", [128, 2, 2, HALF], f16)
        w1 = sb("w1", [128, 2, QUADS * CH], f16)
        wo = sb("wo", [128, TAPS, 2 * OFFS], f16)
        wd = sb("wd", [128, 2, TAPS * CH], f16)
        w2 = sb("w2", [128, 2, QUADS * 128], f16)
        mid = sb("mid", [128, HALF], f32)
        mid_split = sb("mid_split", [128, 2, HALF], f16)
        res = sb("res", [128, 2, HALF], f32)
        eye_sb = sb("eye_sb", [128, 128], f32)
        blocks_sb = sb("blocks_sb", [128, 128], f32)
        fold_sb = sb("fold_sb", [128, GIN], f32)
        ofold_sb = sb("ofold_sb", [2 * OFFS, OFFS], f32)
        grid_sb = sb("grid_sb", [128, 8 * OFFS], f32)
        bias0 = sb("bias0", [128, GROUPS], f32)
        bias_off = sb("bias_off", [128, 1], f32)
        eps_sb = sb("eps_sb", [128, 1], f32)
        bn_sb = sb("bn_sb", [128, 6, 5], f32)
        bn_s = sb("bn_s", [128, 6], f32)
        bn_t = sb("bn_t", [128, 6], f32)
        bn_tmp = sb("bn_tmp", [128, 6], f32)
        raw1 = sb("raw1", [128, 2, 6], f32)
        raw2 = sb("raw2", [128, 2, 6], f32)
        mv = [sb(f"mv{n}", [128, QUADS, 2], f32) for n in (1, 2)]
        gs = [sb(f"gs{n}", [128, QUADS, 6], f32) for n in (1, 2)]
        pos = sb("pos", [128, 8 * OFFS], f32)
        posi = sb("posi", [128, 8 * OFFS], i32)
        posf = sb("posf", [128, 8 * OFFS], f32)
        posg = sb("posg", [128, 8 * OFFS], f32)
        frac = sb("frac", [128, 2, 8, TAPS, 2], f32)
        ridx = sb("ridx", [128, 2, 8, TAPS], i32)

        offs_sb = norm2
        diff = split2[:, :, :, :].rearrange("p a b c -> p (a b c)").bitcast(f32)
        dx, dy, dxy = diff[:, 0:NDX], diff[:, NDX:NDX + ROWS], diff[:, NDX + ROWS:NDX + 2 * ROWS]
        raw_wg = rows[:, :, :].rearrange("p a b -> p (a b)")[:, 0:GROUPS * TAPS * GIN]
        stage = x_mid[:, 1, :, :].rearrange("p a b -> p (a b)")
        ends = [0]
        for n in (QUADS * CH, TAPS * OFFS, TAPS * CH, QUADS * 128):
            ends.append(ends[-1] + n)
        raw_w1, raw_wo, raw_wd, raw_w2 = (stage[:, a:b] for a, b in zip(ends, ends[1:]))

        banks = [ctx.enter_context(nc.psum_tensor(f"bank{n}", [128, 512], f32)) for n in range(8)]
        pair_ps = banks[0:2]
        shuf_ps = banks[2]
        small_ps = banks[3]
        stat_ps = [small_ps[:, 0:2 * QUADS], small_ps[:, 2 * QUADS:4 * QUADS]]
        offT_ps = small_ps[:, 64:64 + 8 * OFFS]
        valT_ps = banks[4:6]
        def_ps = banks[6]
        out_ps = banks[7]

        consts_in = sem("consts_in")
        pool_passed = sem("pool_passed")
        dve_passed = sem("dve_passed")
        zeroed = sem("zeroed")
        w_high = sem("w_high")
        w_low = sem("w_low")
        bn_chain = sem("bn_chain")
        bn_sqrt = sem("bn_sqrt")
        x_loaded = [[sem(f"x_loaded{p}{q}") for q in range(QUADS)] for p in (0, 1)]
        gn_stats = [sem(f"gn{n}_stats") for n in (1, 2)]
        gn_chain = [sem(f"gn{n}_chain") for n in (1, 2)]
        var_chain = [sem(f"gn{n}_var_chain") for n in (1, 2)]
        rs_chain = [sem(f"gn{n}_scale_chain") for n in (1, 2)]
        gn_mean = [sem(f"gn{n}_mean") for n in (1, 2)]
        gn_var = [sem(f"gn{n}_var") for n in (1, 2)]
        gn_sqrt = [sem(f"gn{n}_sqrt") for n in (1, 2)]
        gn_scale = [sem(f"gn{n}_scale") for n in (1, 2)]
        norm_done = [sem(f"norm{n}_done") for n in (1, 2)]
        high_done = [sem(f"high{n}_done") for n in (1, 2)]
        low_done = [sem(f"low{n}_done") for n in (1, 2)]
        conv_done = sem("conv_done")
        conv_out = sem("conv_out")
        shuf_done = sem("shuf_done")
        mid_done = sem("mid_done")
        in_done = sem("in_done")
        h_done = sem("h_done")
        h_high = sem("h_high")
        h_low = sem("h_low")
        diff_done = sem("diff_done")
        tile_done = sem("tile_done")
        tile_out = sem("tile_out")
        tile_stored = [sem(f"tile_stored{n}") for n in (0, 1)]
        off_done = sem("off_done")
        off_out = sem("off_out")
        offT_done = sem("offT_done")
        pos_chain = sem("pos_chain")
        pos_floor = sem("pos_floor")
        pos_done = sem("pos_done")
        gathered = [sem(f"gathered{n}") for n in range(RING)]
        lerp_y = sem("lerp_y")
        val_done = sem("val_done")
        valT_done = sem("valT_done")
        val_high = sem("val_high")
        val_low = sem("val_low")
        def_done = sem("def_done")
        d_out = sem("d_out")
        d_high = sem("d_high")
        d_low = sem("d_low")
        out_done = sem("out_done")
        relu_done = sem("relu_done")
        sum_done = sem("sum_done")
        stored = [sem(f"stored{n}") for n in (0, 1)]

        N_CONSTS = 14

        def count(per, image, n):
            total = image * per + n
            return max(total, 0) if isinstance(image, int) else total

        def stored_tiles(image, parity, tiles):
            total = (image - parity) * (TILES * 16 // 2) + 16 * ((TILES * parity + tiles) // 2)
            return max(total, 0) if isinstance(image, int) else total

        def run(eng, step):
            for t in (-2, -1, 0, 1):
                step(t, t % 2, t >= 1, t >= 0, t >= -1, True)
            with eng.Fori(1, IMAGES // 2 - 1) as j:
                for u in (0, 1):
                    step(2 * j + u, u, True, True, True, True)
            step(IMAGES - 2, 0, True, True, True, False)
            step(IMAGES - 1, 1, True, True, False, False)
            step(IMAGES, 0, True, False, False, False)

        UNITS = [
            [("c", 0, 0), ("c", 0, 1)], [("c", 1, 0), ("c", 1, 1)], [("s", 0, 0), ("c", 2, 0)],
            [("s", 0, 1), ("c", 2, 1)], [("c", 3, 0), ("c", 3, 1)], [("s", 1, 0), ("c", 4, 0)],
            [("s", 1, 1), ("c", 4, 1)], [("c", 5, 0), ("c", 5, 1)], [("s", 2, 0), ("c", 6, 0)],
            [("s", 2, 1), ("c", 6, 1)], [("c", 7, 0), ("c", 7, 1)], [("s", 3, 0)], [("s", 3, 1)],
        ] + [[]] * 5
        TABLE_SLOTS = {14: range(0, 3), 15: range(3, 6), 16: range(6, 9)}

        def plane(ap, row, col, nrows):
            v = ap[:, row * PITCH:(row + nrows) * PITCH]
            return v.rearrange("p (r c) -> p r c", c=PITCH)[:, :, col:col + WIDTH]

        block = ctx.enter_context(nc.Block())

        @block.sync
        def _(sp):
            for dst, src in ((raw_wg[0:64, :], w_group), (raw_wg[64:128, :], w_group), (bias0[0:64, :], b_group),
                             (raw_w1, w_in), (raw_wo, w_off), (bias_off[0:OFFS, :], b_off), (raw_wd, w_def),
                             (raw_w2, w_out), (bn_sb[:, :, :], bn), (eye_sb[:, :], eye), (fold_sb[:, :], fold),
                             (blocks_sb[:, :], blocks), (ofold_sb[:, :], offset_fold), (grid_sb[:, :], grid)):
                sp.wait_ge(zeroed, 1)
                sp.dma_start(dst, src).then_inc(consts_in, 16)

            def step(t, u, tail, b, a2, a1):
                last, nxt, new = t - 1, t + 1, t + 2
                if a1:
                    sp.wait_ge(mid_done, count(2 * QUADS, t, 2 * QUADS))
                    for q in range(QUADS):
                        sp.dma_start(x_in[:, u, q, :], x[bass.ds(new, 1), q].rearrange("a p n -> (a p) n"))\
                          .then_inc(x_loaded[u][q], 16)

                def store(image, half):
                    for q in range(QUADS):
                        sp.wait_ge(sum_done, count(2 * QUADS, image, half * QUADS + q + 1))
                        dst = out[bass.ds(image, 1), q].rearrange("a p n -> (a p) n")
                        sp.dma_start(dst[:, half * HALF:(half + 1) * HALF], res[:, q % 2, :])\
                          .then_inc(stored[q % 2], 16)

                if tail:
                    store(last, 1)
                if b:
                    store(t, 0)
                if a2:
                    for m in range(TILES):
                        sp.wait_ge(tile_out, count(TILES, nxt, m + 1))
                        slot = (m + (u + 1)) % 2
                        sp.dma_start(tables[(u + 1) % 2][m * 128:(m + 1) * 128, :], table_sb[:, slot, :])\
                          .then_inc(tile_stored[slot], 16)

            run(sp, step)
            for n in (0, 1):
                sp.wait_ge(stored[n], 16 * IMAGES * QUADS)

        @block.gpsimd
        def _(pool):
            def step(t, u, tail, b, a2, a1):
                if not b:
                    return
                pool.wait_ge(pos_done, count(1, t, 1))
                for n in (0, 1):
                    pool.wait_ge(tile_stored[n], stored_tiles(t, u, TILES + 1 - n))
                for c in range(CHUNKS):
                    half, k = divmod(c, TAPS)
                    pool.wait_ge(val_done, count(CHUNKS, t, c - RING + 1))
                    pool.sem_inc(pool_passed, 1)
                    for i in range(PER):
                        pool.indirect_dma_start(
                            out=rows[:, (c % RING) * PER + i, :], out_offset=None, in_=tables[u],
                            in_offset=bass.IndirectOffsetOnAxis(
                                ap=ridx[:, u, half * PER + i, k:k + 1].bitcast(u32), axis=0),
                        ).then_inc(gathered[c % RING], 16)

            run(pool, step)

        @block.scalar
        def _(act):
            act.wait_ge(consts_in, 16 * N_CONSTS)
            act.wait_ge(zeroed, 2)
            for g in range(GROUPS):
                nc.scalar.activation(wg[:, g, :, 0:GIN], raw_wg[:, g * TAPS * GIN:(g + 1) * TAPS * GIN]
                                     .rearrange("p (k o) -> p k o", o=GIN), ACT.Copy)
            nc.scalar.activation(w1[:, 0, :], raw_w1, ACT.Copy)
            nc.scalar.activation(wo[:, :, 0:OFFS], raw_wo.rearrange("p (k o) -> p k o", o=OFFS), ACT.Copy)
            nc.scalar.activation(wd[:, 0, :], raw_wd, ACT.Copy)
            nc.scalar.activation(w2[:, 0, :], raw_w2, ACT.Copy).then_inc(w_high, 1)
            nc.scalar.activation(bn_tmp[:, :], bn_sb[:, :, 3], ACT.Sqrt, bias=eps_sb[:, 0:1]).then_inc(bn_sqrt, 1)
            act.wait_ge(bn_chain, 4)

            def step(t, u, tail, b, a2, a1):
                last, nxt, new = t - 1, t + 1, t + 2
                pn = (u + 1) % 2

                def high_part(image, c):
                    act.wait_ge(valT_done, count(CHUNKS, image, c + 1))
                    act.wait_ge(def_done, count(CHUNKS, image, c - 1))
                    nc.scalar.activation(val_split[:, c % 2, 0, :], valT_ps[c % 2][:, :], ACT.Copy)\
                      .then_inc(val_high, 1)

                def deform_out(image, half):
                    act.wait_ge(def_done, count(CHUNKS, image, TAPS * (half + 1)))
                    act.wait_ge(d_low, count(2, image, half))
                    act.wait_ge(out_done, count(2 * QUADS, image, half * QUADS))
                    nc.scalar.activation(mid[:, :], def_ps[:, :], ACT.Identity, bias=bn_t[:, 1:2],
                                         scale=bn_s[:, 1:2]).then_inc(d_out, 1)
                    nc.scalar.activation(mid_split[:, 0, :], def_ps[:, :], ACT.Identity, bias=bn_t[:, 1:2],
                                         scale=bn_s[:, 1:2]).then_inc(d_high, 1)

                def relu_out(image, half, q):
                    act.wait_ge(out_done, count(2 * QUADS, image, half * QUADS + q + 1))
                    n = half * QUADS + q
                    act.wait_ge(stored[q % 2], count(16 * QUADS, image, 16 * (n // 2)))
                    nc.scalar.activation(res[:, q % 2, :], out_ps[:, :], ACT.Relu, bias=bn_t[:, 2 + q:3 + q],
                                         scale=bn_s[:, 2 + q:3 + q]).then_inc(relu_done, 1)

                def conv_to_sbuf(g, half):
                    act.wait_ge(conv_done, count(2 * GROUPS, nxt, 2 * g + half + 1))
                    if g >= 3:
                        act.wait_ge(shuf_done, count(2 * QUADS, nxt, 2 * ((g - 3) // 2) + 2))
                    else:
                        act.wait_ge(shuf_done, count(2 * QUADS, nxt, 0))
                    nc.scalar.activation(conv_sb[:, g % 3, half * HALF:(half + 1) * HALF], pair_ps[half][:, :],
                                         ACT.Identity, bias=bias0[:, g:g + 1]).then_inc(conv_out, 1)

                def gn_root(n, image, q):
                    act.wait_ge(gn_var[n], count(QUADS, image, q + 1))
                    nc.scalar.activation(gs[n][:, q, 2:3], gs[n][:, q, 1:2], ACT.Sqrt, bias=eps_sb[:, 0:1])\
                      .then_inc(gn_sqrt[n], 1)

                def apply1(q):
                    act.wait_ge(gn_scale[0], count(QUADS, new, q + 1))
                    act.wait_ge(low_done[0], count(2 * QUADS, new, 2 * q))
                    scale, shift = gs[0][:, q, 3:4], gs[0][:, q, 4:5]
                    nc.scalar.activation(norm1[:, :], x_in[:, u, q, :], ACT.Identity, bias=shift, scale=scale)\
                      .then_inc(norm_done[0], 1)
                    act.wait_ge(conv_done, count(2 * GROUPS, nxt, 4 * q + 4))
                    for e in (0, 1):
                        p = slice(64 * e, 64 * e + 64)
                        nc.scalar.activation(
                            plane(split1[p, 2 * q + e, :], 1, 1, HEIGHT),
                            x_in[p, u, q, :].rearrange("p (r c) -> p r c", c=WIDTH), ACT.Identity,
                            bias=gs[0][p, q, 4:5], scale=gs[0][p, q, 3:4]).then_inc(high_done[0], 1)

                def apply2(q):
                    act.wait_ge(gn_scale[1], count(QUADS, nxt, q + 1))
                    act.wait_ge(low_done[1], count(QUADS, nxt, q))
                    if q == 0:
                        act.wait_ge(offT_done, count(1, nxt, 0))
                    act.wait_ge(tile_done, count(TILES, nxt, 0))
                    scale, shift = gs[1][:, q, 3:4], gs[1][:, q, 4:5]
                    nc.scalar.activation(norm2[:, :], x_mid[:, pn, q, :], ACT.Identity, bias=shift, scale=scale)\
                      .then_inc(norm_done[1], 1)
                    nc.scalar.activation(split2[:, 0, q, :], x_mid[:, pn, q, :], ACT.Identity, bias=shift,
                                         scale=scale).then_inc(high_done[1], 1)

                for s in range(CHUNKS):
                    if s == 0 and tail:
                        high_part(last, CHUNKS - 1)
                        deform_out(last, 1)
                    if s >= 1 and b:
                        high_part(t, s - 1)
                        if s == TAPS:
                            deform_out(t, 0)
                    if tail and 1 <= s <= QUADS:
                        relu_out(last, 1, s - 1)
                    if b and TAPS + 1 <= s <= TAPS + QUADS:
                        relu_out(t, 0, s - TAPS - 1)
                    convs = [unit for unit in UNITS[s] if unit[0] == "c"] if a2 else []
                    if convs:
                        conv_to_sbuf(*convs[0][1:])
                    if a1 and s % 3 == 1 and s // 3 < QUADS:
                        gn_root(0, new, s // 3)
                    if a2 and s % 3 == 1 and 4 <= s <= 10:
                        gn_root(1, nxt, s // 3 - 1)
                    if a2 and s % 3 == 2 and 5 <= s <= 11:
                        apply2(s // 3 - 1)
                    if a1 and s % 3 == 0 and 3 <= s <= 12:
                        apply1(s // 3 - 1)
                    if a2 and s == 12:
                        gn_root(1, nxt, 3)
                        apply2(3)
                    for unit in convs[1:]:
                        conv_to_sbuf(*unit[1:])
                    if a2 and s == 14:
                        for half in (0, 1):
                            act.wait_ge(in_done, count(2, nxt, half + 1))
                            act.wait_ge(tile_done, count(TILES, nxt, 0))
                            act.wait_ge(h_low, count(1, nxt, 0))
                            act.wait_ge(diff_done, count(3, nxt, 0))
                            nc.scalar.activation(
                                plane(h_sb[:, :], 1 + half * HROWS, 1, HROWS),
                                pair_ps[half][:, :].rearrange("p (r c) -> p r c", c=WIDTH), ACT.Relu,
                                bias=bn_t[:, 0:1], scale=bn_s[:, 0:1]).then_inc(h_done, 1)
                        act.wait_ge(h_done, count(2, nxt, 2))
                        act.wait_ge(off_done, count(2, nxt, 0))
                        nc.scalar.activation(h_split[:, 0, :], h_sb[:, :], ACT.Copy).then_inc(h_high, 1)
                    if a2 and s in TABLE_SLOTS:
                        for m in TABLE_SLOTS[s]:
                            act.wait_ge(tile_done, count(TILES, nxt, m + 1))
                            slot = (m + pn) % 2
                            act.wait_ge(tile_stored[slot], stored_tiles(nxt, pn, m))
                            nc.scalar.activation(table_sb[:, slot, :], shuf_ps[:, :], ACT.Copy).then_inc(tile_out, 1)
                        if s == 16:
                            for half in (0, 1):
                                act.wait_ge(off_done, count(2, nxt, half + 1))
                                act.wait_ge(low_done[1], count(QUADS, nxt, QUADS))
                                nc.scalar.activation(offs_sb[0:2 * OFFS, half * HALF:(half + 1) * HALF],
                                                     pair_ps[half][0:2 * OFFS, :], ACT.Identity,
                                                     bias=bias_off[0:2 * OFFS, 0:1]).then_inc(off_out, 1)

            run(act, step)

        @block.vector
        def _(dve):
            nc.vector.memset(bias0[:, :], 0.0)
            nc.vector.memset(bias_off[:, :], 0.0).then_inc(zeroed, 1)
            nc.vector.memset(split1[:, :, :].rearrange("p a b -> p (a b)").bitcast(f32), 0.0)
            nc.vector.memset(h_sb[:, :], 0.0)
            nc.vector.memset(eps_sb[:, :], EPS).then_inc(zeroed, 1)
            dve.wait_ge(w_high, 1)
            for g in range(GROUPS):
                nc.vector.tensor_tensor(wg[:, g, :, GIN:2 * GIN], raw_wg[:, g * TAPS * GIN:(g + 1) * TAPS * GIN]
                                        .rearrange("p (k o) -> p k o", o=GIN), wg[:, g, :, 0:GIN], ALU.subtract)
            nc.vector.tensor_tensor(w1[:, 1, :], raw_w1, w1[:, 0, :], ALU.subtract)
            nc.vector.tensor_tensor(wo[:, :, OFFS:2 * OFFS], raw_wo.rearrange("p (k o) -> p k o", o=OFFS),
                                    wo[:, :, 0:OFFS], ALU.subtract)
            nc.vector.tensor_tensor(wd[:, 1, :], raw_wd, wd[:, 0, :], ALU.subtract)
            nc.vector.tensor_tensor(w2[:, 1, :], raw_w2, w2[:, 0, :], ALU.subtract).then_inc(w_low, 1)
            dve.wait_ge(bn_sqrt, 1)
            nc.vector.reciprocal(bn_t[:, :], bn_tmp[:, :]).then_inc(bn_chain, 1)
            dve.wait_ge(bn_chain, 1)
            nc.vector.tensor_tensor(bn_s[:, :], bn_t[:, :], bn_sb[:, :, 0], ALU.mult)
            nc.vector.tensor_tensor(bn_tmp[:, :], bn_sb[:, :, 4], bn_sb[:, :, 2], ALU.subtract).then_inc(bn_chain, 1)
            dve.wait_ge(bn_chain, 2)
            nc.vector.tensor_tensor(bn_t[:, :], bn_tmp[:, :], bn_s[:, :], ALU.mult).then_inc(bn_chain, 1)
            dve.wait_ge(bn_chain, 3)
            nc.vector.tensor_tensor(bn_t[:, :], bn_t[:, :], bn_sb[:, :, 1], ALU.add).then_inc(bn_chain, 1)

            def step(t, u, tail, b, a2, a1):
                last, nxt, new = t - 1, t + 1, t + 2
                pn = (u + 1) % 2

                def interpolate(c):
                    half, k = divmod(c, TAPS)
                    first = (c % RING) * PER
                    n = CHUNKS // RING
                    dve.wait_ge(gathered[c % RING], count(16 * PER * n, t, 16 * PER * (c // RING + 1)))
                    for i in range(PER):
                        r = rows[:, first + i, :]
                        last_op = nc.vector.scalar_tensor_tensor(
                            r[:, 0:2 * CH], r[:, 2 * CH:4 * CH], frac[:, u, half * PER + i, k, 0:1], r[:, 0:2 * CH],
                            ALU.mult, ALU.add)
                    last_op.then_inc(lerp_y, 1)
                    dve.wait_ge(lerp_y, count(CHUNKS, t, c + 1))
                    dve.wait_ge(valT_done, count(CHUNKS, t, c - 1))
                    for i in range(PER):
                        r = rows[:, first + i, :]
                        last_op = nc.vector.scalar_tensor_tensor(
                            val[:, c % 2, i * CH:(i + 1) * CH], r[:, CH:2 * CH], frac[:, u, half * PER + i, k, 1:2],
                            r[:, 0:CH], ALU.mult, ALU.add)
                    last_op.then_inc(val_done, 1)

                def low_part(image, c):
                    dve.wait_ge(val_high, count(CHUNKS, image, c + 1))
                    nc.vector.tensor_tensor(val_split[:, c % 2, 1, :], valT_ps[c % 2][:, :],
                                            val_split[:, c % 2, 0, :], ALU.subtract).then_inc(val_low, 1)

                def deform_low(image, half):
                    dve.wait_ge(d_high, count(2, image, half + 1))
                    nc.vector.tensor_tensor(mid_split[:, 1, :], mid[:, :], mid_split[:, 0, :], ALU.subtract)\
                      .then_inc(d_low, 1)

                def add_residual(image, parity, half, q):
                    dve.wait_ge(relu_done, count(2 * QUADS, image, half * QUADS + q + 1))
                    nc.vector.tensor_tensor(res[:, q % 2, :], res[:, q % 2, :],
                                            x_mid[:, parity, q, half * HALF:(half + 1) * HALF], ALU.add)\
                      .then_inc(sum_done, 1)

                def gn_statistics(n, image, q, src, raw):
                    for a in (0, 1):
                        op = nc.vector.bn_stats(raw[:, a, :], src[:, a * HALF:(a + 1) * HALF])
                    op.then_inc(gn_chain[n], 1)
                    dve.wait_ge(gn_chain[n], count(2 * QUADS, image, 2 * q + 1))
                    dve.sem_inc(dve_passed, 1)
                    nc.vector.bn_aggr(mv[n][:, q, :], raw[:, :, :]).then_inc(gn_chain[n], 1)
                    dve.wait_ge(gn_chain[n], count(2 * QUADS, image, 2 * q + 2))
                    nc.vector.scalar_tensor_tensor(mv[n][:, q, 1:2], mv[n][:, q, 0:1], mv[n][:, q, 0:1],
                                                   mv[n][:, q, 1:2], ALU.mult, ALU.add).then_inc(gn_stats[n], 1)

                def gn_variance(n, image, q):
                    dve.wait_ge(gn_mean[n], count(QUADS, image, q + 1))
                    g = gs[n]
                    nc.vector.tensor_copy(g[:, q, 0:2], stat_ps[n][:, 2 * q:2 * q + 2]).then_inc(var_chain[n], 1)
                    dve.wait_ge(var_chain[n], count(2 * QUADS, image, 2 * q + 1))
                    nc.vector.tensor_scalar(g[:, q, 5:6], g[:, q, 0:1], g[:, q, 0:1], -1.0, ALU.mult, ALU.mult)\
                      .then_inc(var_chain[n], 1)
                    dve.wait_ge(var_chain[n], count(2 * QUADS, image, 2 * q + 2))
                    nc.vector.tensor_tensor(g[:, q, 1:2], g[:, q, 5:6], g[:, q, 1:2], ALU.add).then_inc(gn_var[n], 1)

                def gn_scales(n, image, q):
                    dve.wait_ge(gn_sqrt[n], count(QUADS, image, q + 1))
                    g = gs[n]
                    nc.vector.reciprocal(g[:, q, 3:4], g[:, q, 2:3]).then_inc(rs_chain[n], 1)
                    dve.wait_ge(rs_chain[n], count(QUADS, image, q + 1))
                    nc.vector.tensor_scalar(g[:, q, 4:5], g[:, q, 0:1], g[:, q, 3:4], -1.0, ALU.mult, ALU.mult)\
                      .then_inc(gn_scale[n], 1)

                def low1(q):
                    for e in (0, 1):
                        p, o = slice(64 * e, 64 * e + 64), slice(64 - 64 * e, 128 - 64 * e)
                        dve.wait_ge(high_done[0], count(2 * QUADS, new, 2 * q + e + 1))
                        nc.vector.tensor_tensor(
                            plane(split1[o, 2 * q + e, :], 1, 1, HEIGHT),
                            norm1[p, :].rearrange("p (r c) -> p r c", c=WIDTH),
                            plane(split1[p, 2 * q + e, :], 1, 1, HEIGHT), ALU.subtract).then_inc(low_done[0], 1)

                def low2(q):
                    dve.wait_ge(high_done[1], count(QUADS, nxt, q + 1))
                    nc.vector.tensor_tensor(split2[:, 1, q, :], norm2[:, :], split2[:, 0, q, :], ALU.subtract)\
                      .then_inc(low_done[1], 1)

                def coordinates():
                    dve.wait_ge(offT_done, count(1, nxt, 1))
                    links = [0]

                    def link(op):
                        links[0] += 1
                        op.then_inc(pos_chain, 1)
                        dve.wait_ge(pos_chain, count(6, nxt, links[0]))

                    link(nc.vector.tensor_tensor(pos[:, :], offT_ps[:, :], grid_sb[:, :], ALU.add))
                    link(nc.vector.tensor_scalar(pos[:, :], pos[:, :], -1.0, float(HEIGHT), ALU.max, ALU.min))
                    link(nc.vector.tensor_copy(posi[:, :], pos[:, :]))
                    link(nc.vector.tensor_copy(posf[:, :], posi[:, :]))
                    link(nc.vector.tensor_tensor(posg[:, :], posf[:, :], pos[:, :], ALU.is_gt))
                    link(nc.vector.tensor_tensor(posf[:, :], posf[:, :], posg[:, :], ALU.subtract))
                    nc.vector.tensor_scalar(posf[:, :], posf[:, :], float(HEIGHT - 1), None, ALU.min)\
                      .then_inc(pos_floor, 1)
                    dve.wait_ge(pos_floor, count(2, nxt, 1))
                    nc.vector.tensor_tensor(frac[:, pn, :, :, :].rearrange("p a b c -> p (a b c)"), pos[:, :],
                                            posf[:, :], ALU.subtract)
                    yx = posf[:, :].rearrange("p (a b c) -> p a b c", b=TAPS, c=2)
                    g0 = posg[:, 0:8 * TAPS].rearrange("p (a b) -> p a b", b=TAPS)
                    nc.vector.scalar_tensor_tensor(g0, yx[:, :, :, 0], float(PITCH), yx[:, :, :, 1], ALU.mult,
                                                   ALU.add).then_inc(pos_floor, 1)
                    dve.wait_ge(pos_floor, count(2, nxt, 2))
                    nc.vector.tensor_scalar(ridx[:, pn, :, :], g0, float(PITCH + 1), None, ALU.add)\
                      .then_inc(pos_done, 1)

                def add_shuffled(q, half):
                    dve.wait_ge(shuf_done, count(2 * QUADS, nxt, 2 * q + half + 1))
                    h = slice(half * HALF, (half + 1) * HALF)
                    nc.vector.tensor_tensor(x_mid[:, pn, q, h], shuf_ps[:, :], x_in[:, pn, q, h], ALU.add)\
                      .then_inc(mid_done, 1)

                for s in range(CHUNKS):
                    if b:
                        interpolate(s)
                    if s == 0 and tail:
                        low_part(last, CHUNKS - 1)
                        deform_low(last, 1)
                    if s >= 1 and b:
                        low_part(t, s - 1)
                        if s == TAPS:
                            deform_low(t, 0)
                    if a1 and s % 3 == 1 and s // 3 < QUADS:
                        gn_variance(0, new, s // 3)
                    if a2 and s % 3 == 1 and 4 <= s <= 10:
                        gn_variance(1, nxt, s // 3 - 1)
                    if a1 and s % 3 == 2 and s // 3 < QUADS:
                        gn_scales(0, new, s // 3)
                    if a2 and s % 3 == 2 and 5 <= s <= 11:
                        gn_scales(1, nxt, s // 3 - 1)
                    if a2 and s % 3 == 0 and 6 <= s <= 12:
                        low2(s // 3 - 2)
                    if a1 and s % 3 == 0 and s // 3 < QUADS:
                        dve.wait_ge(x_loaded[u][s // 3], (new - u) * 8 + 16)
                        gn_statistics(0, new, s // 3, x_in[:, u, s // 3, :], raw1)
                    if a1 and s % 3 == 1 and 4 <= s <= 13:
                        low1(s // 3 - 1)
                    if tail and 1 <= s <= QUADS:
                        add_residual(last, pn, 1, s - 1)
                    if b and TAPS + 1 <= s <= TAPS + QUADS:
                        add_residual(t, u, 0, s - TAPS - 1)
                    for unit in UNITS[s] if a2 else []:
                        if unit[0] == "s":
                            _, q, half = unit
                            add_shuffled(q, half)
                            if half == 1:
                                dve.wait_ge(mid_done, count(2 * QUADS, nxt, 2 * q + 2))
                                gn_statistics(1, nxt, q, x_mid[:, pn, q, :], raw2)
                    if a2 and s == 12:
                        gn_variance(1, nxt, 3)
                        gn_scales(1, nxt, 3)
                        low2(3)
                    if a2 and s == 14:
                        dve.wait_ge(h_done, count(2, nxt, 2))
                        nc.vector.tensor_tensor(dx, h_sb[:, 1:NDX + 1], h_sb[:, 0:NDX], ALU.subtract)
                        nc.vector.tensor_tensor(dy, h_sb[:, PITCH:PITCH + ROWS], h_sb[:, 0:ROWS], ALU.subtract)\
                          .then_inc(diff_done, 1)
                        dve.wait_ge(diff_done, count(3, nxt, 1))
                        nc.vector.tensor_tensor(dxy, dx[:, PITCH:PITCH + ROWS], dx[:, 0:ROWS], ALU.subtract)\
                          .then_inc(diff_done, 2)
                        dve.wait_ge(h_high, count(1, nxt, 1))
                        nc.vector.tensor_tensor(h_split[:, 1, :], h_sb[:, :], h_split[:, 0, :], ALU.subtract)\
                          .then_inc(h_low, 1)
                    if a2 and s == 17:
                        coordinates()

            run(dve, step)

        @block.tensor
        def _(pe):
            pe.wait_ge(w_low, 1)

            def step(t, u, tail, b, a2, a1):
                last, nxt, new = t - 1, t + 1, t + 2

                def transpose_values(c):
                    pe.wait_ge(val_done, count(CHUNKS, t, c + 1))
                    pe.wait_ge(val_low, count(CHUNKS, t, c - 1))
                    for i in range(PER):
                        op = nc.tensor.transpose(valT_ps[c % 2][:, i * CH:(i + 1) * CH],
                                                 val[:, c % 2, i * CH:(i + 1) * CH], eye_sb[:, :])
                    op.then_inc(valT_done, 1)

                def deform(image, c):
                    half, k = divmod(c, TAPS)
                    pe.wait_ge(val_low, count(CHUNKS, image, c + 1))
                    if k == 0:
                        pe.wait_ge(d_high, count(2, image, half))
                    w = slice(k * CH, (k + 1) * CH)
                    v = val_split[:, c % 2, :, :]
                    nc.tensor.matmul(def_ps[:, :], wd[:, 0, w], v[:, 0, :], start=k == 0, stop=False)
                    nc.tensor.matmul(def_ps[:, :], wd[:, 0, w], v[:, 1, :], start=False, stop=False)
                    nc.tensor.matmul(def_ps[:, :], wd[:, 1, w], v[:, 0, :], start=False, stop=k == TAPS - 1)\
                      .then_inc(def_done, 1)

                def out_conv(image, half, q):
                    if q == 0:
                        pe.wait_ge(d_low, count(2, image, half + 1))
                    pe.wait_ge(relu_done, count(2 * QUADS, image, half * QUADS + q))
                    w = slice(q * 128, (q + 1) * 128)
                    nc.tensor.matmul(out_ps[:, :], w2[:, 0, w], mid_split[:, 0, :], start=True, stop=False)
                    nc.tensor.matmul(out_ps[:, :], w2[:, 0, w], mid_split[:, 1, :], start=False, stop=False)
                    nc.tensor.matmul(out_ps[:, :], w2[:, 1, w], mid_split[:, 0, :], start=False, stop=True)\
                      .then_inc(out_done, 1)

                def small_bank_read(q1, q2):
                    if a1:
                        pe.wait_ge(gn_var[0], count(QUADS, new, q1))
                    if a2:
                        pe.wait_ge(gn_var[1], count(QUADS, nxt, q2))

                def gn_average(n, image, q):
                    pe.wait_ge(gn_stats[n], count(QUADS, image, q + 1))
                    if q == 0:
                        pe.wait_ge(pos_done, count(1, nxt, 0))
                    if n == 0:
                        small_bank_read(q, max(q - 1, 0))
                    else:
                        small_bank_read(min(q + 2, QUADS), q)
                    nc.tensor.matmul(stat_ps[n][:, 2 * q:2 * q + 2], blocks_sb[:, :], mv[n][:, q, :], start=True,
                                     stop=True).then_inc(gn_mean[n], 1)

                def group_conv(g, half):
                    pe.wait_ge(low_done[0], count(2 * QUADS, nxt, g + 1))
                    n = 2 * g + half
                    if n >= 2:
                        pe.wait_ge(conv_out, count(2 * GROUPS, nxt, n - 1))
                    else:
                        pe.wait_ge(off_out, count(2, nxt, 0))
                    for k in range(TAPS):
                        ky, kx = divmod(k, 3)
                        op = nc.tensor.matmul(pair_ps[half][:, :], wg[:, g, k, :],
                                              plane(split1[:, g, :], ky + half * HROWS, kx, HROWS),
                                              start=k == 0, stop=k == TAPS - 1)
                    op.then_inc(conv_done, 1)

                def shuffle(q, half):
                    pe.wait_ge(conv_out, count(2 * GROUPS, nxt, 4 * q + 4))
                    if q == half == 0:
                        pe.wait_ge(tile_out, count(TILES, nxt, 0))
                    else:
                        pe.wait_ge(mid_done, count(2 * QUADS, nxt, 2 * q + half))
                    for e in (0, 1):
                        for jj in range(COLS // 2):
                            j = half * (COLS // 2) + jj
                            op = nc.tensor.matmul(
                                shuf_ps[64 * e:64 * e + 64, jj * GIN:(jj + 1) * GIN],
                                conv_sb[:, (2 * q + e) % 3, j:j + COLS * (GIN - 1) + 1:COLS], fold_sb[:, :],
                                start=True, stop=True)
                    op.then_inc(shuf_done, 1)

                def in_conv(q):
                    pe.wait_ge(low_done[1], count(QUADS, nxt, q + 1))
                    for half in (0, 1):
                        if q == 0:
                            pe.wait_ge(conv_out, count(2 * GROUPS, nxt, 2 * GROUPS - 1 + half))
                        w = slice(q * CH, (q + 1) * CH)
                        h = slice(half * HALF, (half + 1) * HALF)
                        ps = pair_ps[half]
                        nc.tensor.matmul(ps[:, :], w1[:, 0, w], split2[:, 0, q, h], start=q == 0, stop=False)
                        nc.tensor.matmul(ps[:, :], w1[:, 0, w], split2[:, 1, q, h], start=False, stop=False)
                        op = nc.tensor.matmul(ps[:, :], w1[:, 1, w], split2[:, 0, q, h], start=False,
                                              stop=q == QUADS - 1)
                        if q == QUADS - 1:
                            op.then_inc(in_done, 1)

                def table_tile(m):
                    pe.wait_ge(tile_out, count(TILES, nxt, m))
                    if m == 0:
                        pe.wait_ge(mid_done, count(2 * QUADS, nxt, 2 * QUADS))
                        pe.wait_ge(diff_done, count(3, nxt, 3))
                    r = slice(m * 128, (m + 1) * 128)
                    for i, src in enumerate((h_sb[:, r], dx[:, r], dy[:, r], dxy[:, r])):
                        op = nc.tensor.transpose(shuf_ps[:, i * CH:(i + 1) * CH], src, eye_sb[:, :])
                    op.then_inc(tile_done, 1)

                def offset_conv(m):
                    for n in range(4 * m, 4 * m + 4):
                        half, r = divmod(n, 2 * TAPS)
                        k, part = divmod(r, 2)
                        ky, kx = divmod(k, 3)
                        if n == 0:
                            pe.wait_ge(h_high, count(1, nxt, 1))
                            pe.wait_ge(h_low, count(1, nxt, 1))
                        op = nc.tensor.matmul(pair_ps[half][0:2 * OFFS, :], wo[:, k, :],
                                              plane(h_split[:, part, :], ky + half * HROWS, kx, HROWS),
                                              start=r == 0, stop=r == 2 * TAPS - 1)
                        if r == 2 * TAPS - 1:
                            op.then_inc(off_done, 1)

                for s in range(CHUNKS):
                    if b:
                        transpose_values(s)
                    if s == 0 and tail:
                        deform(last, CHUNKS - 1)
                    if s >= 1 and b:
                        deform(t, s - 1)
                    if tail and 1 <= s <= QUADS:
                        out_conv(last, 1, s - 1)
                    if b and TAPS + 1 <= s <= TAPS + QUADS:
                        out_conv(t, 0, s - TAPS - 1)
                    if a1 and s % 3 == 1 and s // 3 < QUADS:
                        gn_average(0, new, s // 3)
                    if a2 and s % 3 == 1 and 4 <= s <= 10:
                        gn_average(1, nxt, s // 3 - 1)
                    for unit in UNITS[s] if a2 else []:
                        (group_conv if unit[0] == "c" else shuffle)(*unit[1:])
                    if a2 and s == 11:
                        in_conv(0)
                        in_conv(1)
                    if a2 and s == 12:
                        gn_average(1, nxt, 3)
                        in_conv(2)
                    if a2 and s == 13:
                        in_conv(3)
                    if a2 and s in TABLE_SLOTS:
                        for m in TABLE_SLOTS[s]:
                            table_tile(m)
                            offset_conv(m)
                    if a2 and s == 17:
                        pe.wait_ge(off_out, count(2, nxt, 2))
                        for i in range(8):
                            op = nc.tensor.matmul(offT_ps[:, i * OFFS:(i + 1) * OFFS],
                                                  offs_sb[0:2 * OFFS, i * 128:(i + 1) * 128], ofold_sb[:, :],
                                                  start=True, stop=True)
                        op.then_inc(offT_done, 1)

            run(pe, step)


def constants():
    import numpy as np

    eye = np.eye(128, dtype=np.float32)
    fold = np.concatenate([np.eye(64, dtype=np.float32)] * 2)
    blocks = np.kron(np.eye(8, dtype=np.float32), np.full((16, 16), 1 / 16, np.float32))
    offset_fold = np.concatenate([np.eye(18, dtype=np.float32)] * 2)
    grid = np.zeros((128, 8, 9, 2), np.float32)
    for p in range(128):
        for i in range(8):
            for k in range(9):
                y, x = divmod(i * 128 + p, 32)
                grid[p, i, k] = (y + k // 3 - 1, x + k % 3 - 1)
    return eye, fold, blocks, offset_fold, grid.reshape(128, -1)


def kernel(x, L0_conv_W, L0_conv_b, L1_conv_conv1_w, L1_conv_conv1_b, L1_conv_bn1_g, L1_conv_bn1_b, L1_conv_bn1_m,
           L1_conv_bn1_v, L1_conv_off_w, L1_conv_off_b, L1_conv_dconv_w, L1_conv_dconv_b, L1_conv_bn2_g,
           L1_conv_bn2_b, L1_conv_bn2_m, L1_conv_bn2_v, L1_conv_conv2_w, L1_conv_conv2_b, L1_conv_bn3_g,
           L1_conv_bn3_b, L1_conv_bn3_m, L1_conv_bn3_v):
    import numpy as np
    import concourse.bacc as bacc
    from concourse.bass_utils import run_bass_kernel_spmd

    def wide(*vectors):
        return np.stack([np.asarray(v).reshape(-1, 128).T for v in vectors], axis=-1)

    eye, fold, blocks, offset_fold, grid = constants()
    bn = np.concatenate([
        wide(L1_conv_bn1_g, L1_conv_bn1_b, L1_conv_bn1_m, L1_conv_bn1_v, L1_conv_conv1_b),
        wide(L1_conv_bn2_g, L1_conv_bn2_b, L1_conv_bn2_m, L1_conv_bn2_v, L1_conv_dconv_b),
        wide(L1_conv_bn3_g, L1_conv_bn3_b, L1_conv_bn3_m, L1_conv_bn3_v, L1_conv_conv2_b)], axis=1)
    arrays = {
        "x": np.asarray(x).reshape(16, 4, 128, 1024),
        "w_group": np.asarray(L0_conv_W).reshape(8, 64, 64, 9).transpose(2, 0, 3, 1).reshape(64, -1),
        "b_group": np.asarray(L0_conv_b).T,
        "w_in": np.asarray(L1_conv_conv1_w).T.reshape(4, 128, 128).transpose(1, 0, 2).reshape(128, -1),
        "w_off": np.asarray(L1_conv_off_w).reshape(18, 128, 9).transpose(1, 2, 0).reshape(128, -1),
        "b_off": np.asarray(L1_conv_off_b).reshape(18, 1),
        "w_def": np.asarray(L1_conv_dconv_w).reshape(128, 128, 9).transpose(1, 2, 0).reshape(128, -1),
        "w_out": np.asarray(L1_conv_conv2_w).T,
        "bn": bn, "eye": eye, "fold": fold, "blocks": blocks, "offset_fold": offset_fold, "grid": grid,
    }
    arrays = {name: np.ascontiguousarray(a) for name, a in arrays.items()}
    nc = bacc.Bacc("TRN2", target_bir_lowering=False, num_devices=1)
    args = [nc.dram_tensor(name, a.shape, mybir.dt.from_np(a.dtype), kind="ExternalInput").ap()
            for name, a in arrays.items()]
    tables = [nc.dram_tensor(f"table{n}", (9 * 128, 512), mybir.dt.float32, kind="Internal").ap() for n in (0, 1)]
    out = nc.dram_tensor("out", (16, 4, 128, 1024), mybir.dt.float32, kind="ExternalOutput").ap()
    build_program(nc, *args, tables, out)
    r = run_bass_kernel_spmd(nc, [arrays], core_ids=[0])
    return r.results[0]["out"].reshape(16, 512, 32, 32)
```

```python
import concourse.bass as bass
from concourse import mybir
from contextlib import ExitStack


def build_program(nc, x, w_group, b_group, w_in, w_off, b_off, w_def, w_out, bn, eye, fold, blocks, offset_fold,
                  grid, tables, out):
    f32, f16, i32, u32 = mybir.dt.float32, mybir.dt.float16, mybir.dt.int32, mybir.dt.uint32
    ALU = mybir.AluOpType
    ACT = mybir.ActivationFunctionType

    IMAGES, CHANNELS, HEIGHT, WIDTH = 16, 512, 32, 32
    PIX = HEIGHT * WIDTH
    HALF = PIX // 2
    HROWS = HEIGHT // 2
    QUADS = CHANNELS // 128
    GROUPS = 8
    GIN = CHANNELS // GROUPS
    TAPS = 9
    PITCH = WIDTH + 2
    PLANE = PITCH * (HEIGHT + 2)
    TILES = 9
    ROWS = TILES * 128
    HPLANE = PITCH * (HEIGHT + 3)
    NDX = ROWS + PITCH
    CH = 128
    OFFS = 2 * TAPS
    CHUNKS = 2 * TAPS
    SHIFT = 2
    RING = 3
    TBUFS = 3
    PER = 4
    ROW = 4 * CH
    COLS = PIX // GIN
    EPS = 1e-5

    ctx = ExitStack()
    with ctx:
        def sb(name, shape, dt):
            return ctx.enter_context(nc.sbuf_tensor("sb_" + name, shape, dt))

        def sem(name):
            return ctx.enter_context(nc.semaphore(name))

        x_in = sb("x_in", [128, 2, QUADS, PIX], f32)
        x_mid = sb("x_mid", [128, 2, QUADS, PIX], f32)
        split1 = sb("split1", [128, GROUPS, PLANE], f16)
        wg = sb("wg", [128, GROUPS, TAPS, 2 * GIN], f16)
        conv_sb = sb("conv_sb", [128, 3, PIX], f32)
        norm1 = sb("norm1", [128, PIX], f32)
        diff = sb("diff", [128, NDX + 2 * ROWS], f32)
        h_sb = sb("h_sb", [128, HPLANE], f32)
        h_split = sb("h_split", [128, 2, HPLANE], f16)
        table_sb = sb("table_sb", [128, TBUFS, ROW], f32)
        rows = sb("rows", [128, RING * PER, ROW], f32)
        val = sb("val", [128, 2, PER * CH], f32)
        valT = sb("valT", [128, 2, HALF], f32)
        w1 = sb("w1", [128, QUADS * CH], f32)
        w1_norm = sb("w1_norm", [128, QUADS * CH], f32)
        wo = sb("wo", [128, TAPS, 2 * OFFS], f16)
        wd = sb("wd", [128, TAPS * CH], f32)
        w2 = sb("w2", [128, QUADS * 128], f32)
        mid = sb("mid", [128, HALF], f32)
        res = sb("res", [128, QUADS, HALF], f32)
        eye_sb = sb("eye_sb", [128, 128], f32)
        blocks_sb = sb("blocks_sb", [128, 128], f32)
        fold_sb = sb("fold_sb", [128, GIN], f32)
        ofold_sb = sb("ofold_sb", [2 * OFFS, OFFS], f32)
        grid_sb = sb("grid_sb", [128, 8 * OFFS], f32)
        bias0 = sb("bias0", [128, GROUPS], f32)
        bias_off = sb("bias_off", [128, 1], f32)
        eps_sb = sb("eps_sb", [128, 1], f32)
        bn_sb = sb("bn_sb", [128, 6, 5], f32)
        bn_s = sb("bn_s", [128, 6], f32)
        bn_t = sb("bn_t", [128, 6], f32)
        bn_tmp = sb("bn_tmp", [128, 6], f32)
        raw2 = sb("raw2", [128, 2, 6], f32)
        sums1 = sb("sums1", [128, 2, QUADS], f32)
        mv2 = sb("mv2", [128, QUADS, 2], f32)
        gs1 = sb("gs1", [128, 6, QUADS], f32)
        gs2 = sb("gs2", [128, QUADS, 6], f32)
        h_bias = sb("h_bias", [128, 1], f32)
        pos = sb("pos", [128, 8 * OFFS], f32)
        posi = sb("posi", [128, 8 * OFFS], i32)
        posf = sb("posf", [128, 8 * OFFS], f32)
        posg = sb("posg", [128, 8 * OFFS], f32)
        frac = sb("frac", [128, 2, 8, TAPS, 2], f32)
        ridx = sb("ridx", [128, 2, 8, TAPS], i32)

        dx, dy, dxy = diff[:, 0:NDX], diff[:, NDX:NDX + ROWS], diff[:, NDX + ROWS:NDX + 2 * ROWS]
        offs_sb = conv_sb[0:2 * OFFS, 2, :]
        raw_wg = rows[:, :, :].rearrange("p a b -> p (a b)")[:, 0:GROUPS * TAPS * GIN]
        raw_wo = norm1[:, 0:TAPS * OFFS]

        banks = [ctx.enter_context(nc.psum_tensor(f"bank{n}", [128, 512], f32)) for n in range(8)]
        pair_ps = banks[0:2]
        shuf_ps = banks[2]
        small_ps = banks[3]
        stat1_ps = small_ps[:, 0:2 * QUADS]
        stat2_ps = small_ps[:, 2 * QUADS:4 * QUADS]
        shift_ps = small_ps[:, 32:33]
        offT_ps = small_ps[:, 64:64 + 8 * OFFS]
        valT_ps = banks[4:6]
        def_ps = banks[6]
        out_ps = banks[7]

        consts_in = sem("consts_in")
        pool_passed = sem("pool_passed")
        dve_passed = sem("dve_passed")
        zeroed = sem("zeroed")
        w_high = sem("w_high")
        w_low = sem("w_low")
        bn_chain = sem("bn_chain")
        bn_sqrt = sem("bn_sqrt")
        x_loaded = [[sem(f"x_loaded{p}{q}") for q in range(QUADS)] for p in (0, 1)]
        sums_done = sem("sums_done")
        mean1_done = sem("mean1_done")
        read1_done = sem("read1_done")
        chain1 = sem("chain1")
        var1_done = sem("var1_done")
        root1_done = sem("root1_done")
        scale1_done = sem("scale1_done")
        norm1_done = sem("norm1_done")
        low1_done = sem("low1_done")
        stats2_done = sem("stats2_done")
        agg2_chain = sem("agg2_chain")
        mean2_done = sem("mean2_done")
        read2_done = sem("read2_done")
        square2 = sem("square2")
        recip2 = sem("recip2")
        var2_done = sem("var2_done")
        root2_done = sem("root2_done")
        scale2_done = sem("scale2_done")
        w1_done = sem("w1_done")
        shift_done = sem("shift_done")
        bias_done = sem("bias_done")
        conv_done = sem("conv_done")
        conv_out = sem("conv_out")
        shuf_done = sem("shuf_done")
        mid_done = sem("mid_done")
        in_done = sem("in_done")
        h_done = sem("h_done")
        h_high = sem("h_high")
        h_low = sem("h_low")
        diff_done = sem("diff_done")
        tile_done = sem("tile_done")
        tile_out = sem("tile_out")
        tile_stored = [sem(f"tile_stored{n}") for n in range(TBUFS)]
        off_done = sem("off_done")
        off_out = sem("off_out")
        offT_done = sem("offT_done")
        pos_chain = sem("pos_chain")
        pos_floor = sem("pos_floor")
        pos_done = sem("pos_done")
        gathered = [sem(f"gathered{n}") for n in range(RING)]
        lerp_y = sem("lerp_y")
        val_done = sem("val_done")
        valT_done = sem("valT_done")
        val_out = sem("val_out")
        def_done = sem("def_done")
        d_out = sem("d_out")
        out_done = sem("out_done")
        relu_done = sem("relu_done")
        sum_done = sem("sum_done")
        stored = [sem(f"stored{n}") for n in range(QUADS)]

        N_CONSTS = 14

        def count(per, image, n):
            total = image * per + n
            return max(total, 0) if isinstance(image, int) else total

        def run(eng, step):
            for t in (-2, -1, 0, 1):
                step(t, t % 2, t >= 1, t >= 0, t >= -1, True)
            with eng.Fori(1, IMAGES // 2 - 1) as j:
                for u in (0, 1):
                    step(2 * j + u, u, True, True, True, True)
            step(IMAGES - 2, 0, True, True, True, False)
            step(IMAGES - 1, 1, True, True, False, False)
            step(IMAGES, 0, True, False, False, False)

        UNITS = [
            [("c", 0, 0), ("c", 0, 1)], [("c", 1, 0), ("c", 1, 1)], [("c", 2, 0), ("s", 0, 0)],
            [("c", 2, 1), ("c", 3, 0)], [("s", 0, 1), ("c", 3, 1)], [("c", 4, 0), ("s", 1, 0)],
            [("c", 4, 1), ("s", 1, 1)], [("c", 5, 0), ("c", 5, 1)], [("c", 6, 0), ("s", 2, 0)],
            [("c", 6, 1), ("s", 2, 1)], [("c", 7, 0), ("c", 7, 1)], [("s", 3, 0)], [("s", 3, 1)],
        ] + [[]] * 5
        MEAN2, VAR2, ROOT2, SCALE2, W1 = (5, 7, 10, 12), (6, 8, 11, 12), (7, 9, 11, 13), (8, 10, 12, 13), (9, 11, 12, 13)
        IN_CONV = {11: (0,), 12: (1,), 13: (2, 3)}
        DIFF_SLOT = 14
        TABLE_SLOTS = {15: range(0, 3), 16: range(3, 6), 17: range(6, 9)}
        SUM_SLOTS = (2, 3, 4, 5)
        APPLY_SLOTS = (8, 9, 10, 12)

        def plane(ap, row, col, nrows):
            v = ap[:, row * PITCH:(row + nrows) * PITCH]
            return v.rearrange("p (r c) -> p r c", c=PITCH)[:, :, col:col + WIDTH]

        block = ctx.enter_context(nc.Block())

        @block.sync
        def _(sp):
            sp.wait_ge(zeroed, 1)
            for dst, src in ((raw_wg[0:64, :], w_group), (raw_wg[64:128, :], w_group), (bias0[0:64, :], b_group),
                             (w1[:, :], w_in), (raw_wo, w_off), (bias_off[0:OFFS, :], b_off), (wd[:, :], w_def),
                             (w2[:, :], w_out), (bn_sb[:, :, :], bn), (eye_sb[:, :], eye), (fold_sb[:, :], fold),
                             (blocks_sb[:, :], blocks), (ofold_sb[:, :], offset_fold), (grid_sb[:, :], grid)):
                sp.dma_start(dst, src).then_inc(consts_in, 16)

            def step(t, u, tail, b, a2, a1):
                last, nxt, new = t - 1, t + 1, t + 2

                def store(image, half, q):
                    sp.wait_ge(sum_done, count(2 * QUADS, image, half * QUADS + q + 1))
                    dst = out[bass.ds(image, 1), q].rearrange("a p n -> (a p) n")
                    sp.dma_start(dst[:, half * HALF:(half + 1) * HALF], res[:, q, :]).then_inc(stored[q], 16)

                if a1:
                    sp.wait_ge(mid_done, count(2 * QUADS, t, 2 * QUADS))
                    for q in range(QUADS):
                        sp.dma_start(x_in[:, u, q, :], x[bass.ds(new, 1), q].rearrange("a p n -> (a p) n"))\
                          .then_inc(x_loaded[u][q], 16)
                for q in range(QUADS if tail else 0):
                    store(last, 1, q)
                for s in range(CHUNKS):
                    for m in TABLE_SLOTS.get(s, ()) if a2 else ():
                        sp.wait_ge(tile_out, count(TILES, nxt, m + 1))
                        sp.dma_start(tables[(u + 1) % 2][m * 128:(m + 1) * 128, :], table_sb[:, m % TBUFS, :])\
                          .then_inc(tile_stored[m % TBUFS], 16)
                    if b and 0 <= s - SHIFT - 3 - TAPS + 1 < QUADS:
                        store(t, 0, s - SHIFT - 3 - TAPS + 1)

            run(sp, step)
            for q in range(QUADS):
                sp.wait_ge(stored[q], 16 * IMAGES * 2)

        @block.gpsimd
        def _(pool):
            def step(t, u, tail, b, a2, a1):
                if not b:
                    return
                pool.wait_ge(pos_done, count(1, t, 1))
                for n in range(TBUFS):
                    pool.wait_ge(tile_stored[n], count(16 * TILES // TBUFS, t, 16 * TILES // TBUFS))
                for c in range(CHUNKS):
                    half, k = divmod(c, TAPS)
                    pool.wait_ge(val_done, count(CHUNKS, t, c - RING + 1))
                    pool.sem_inc(pool_passed, 1)
                    for i in range(PER):
                        pool.indirect_dma_start(
                            out=rows[:, (c % RING) * PER + i, :], out_offset=None, in_=tables[u],
                            in_offset=bass.IndirectOffsetOnAxis(
                                ap=ridx[:, u, half * PER + i, k:k + 1].bitcast(u32), axis=0),
                        ).then_inc(gathered[c % RING], 16)

            run(pool, step)

        @block.scalar
        def _(act):
            act.wait_ge(consts_in, 16 * N_CONSTS)
            act.wait_ge(zeroed, 2)
            nc.scalar.activation(bn_tmp[:, :], bn_sb[:, :, 3], ACT.Sqrt, bias=eps_sb[:, 0:1]).then_inc(bn_sqrt, 1)
            for g in range(GROUPS):
                nc.scalar.activation(wg[:, g, :, 0:GIN], raw_wg[:, g * TAPS * GIN:(g + 1) * TAPS * GIN]
                                     .rearrange("p (k o) -> p k o", o=GIN), ACT.Copy)
            nc.scalar.activation(wo[:, :, 0:OFFS], raw_wo.rearrange("p (k o) -> p k o", o=OFFS), ACT.Copy)\
              .then_inc(w_high, 1)
            act.wait_ge(w_low, 1)
            act.wait_ge(bn_chain, 4)

            def step(t, u, tail, b, a2, a1):
                last, nxt, new = t - 1, t + 1, t + 2
                pn = (u + 1) % 2

                def chunk_at(s, lag):
                    v = s - SHIFT - lag
                    if v >= 0:
                        return (t, v) if b else (None, None)
                    return (last, v + CHUNKS) if tail and v + CHUNKS >= 0 else (None, None)

                def value_out(image, c):
                    act.wait_ge(valT_done, count(CHUNKS, image, c + 1))
                    act.wait_ge(def_done, count(CHUNKS, image, c - 1))
                    nc.scalar.activation(valT[:, c % 2, :], valT_ps[c % 2][:, :], ACT.Copy).then_inc(val_out, 1)

                def deform_out(image, half):
                    act.wait_ge(def_done, count(CHUNKS, image, TAPS * (half + 1)))
                    act.wait_ge(out_done, count(2 * QUADS, image, half * QUADS))
                    nc.scalar.activation(mid[:, :], def_ps[:, :], ACT.Identity, bias=bn_t[:, 1:2],
                                         scale=bn_s[:, 1:2]).then_inc(d_out, 1)

                def relu_out(image, half, q):
                    act.wait_ge(out_done, count(2 * QUADS, image, half * QUADS + q + 1))
                    act.wait_ge(stored[q], count(32, image, 16 * half))
                    nc.scalar.activation(res[:, q, :], out_ps[:, :], ACT.Relu, bias=bn_t[:, 2 + q:3 + q],
                                         scale=bn_s[:, 2 + q:3 + q]).then_inc(relu_done, 1)

                def conv_to_sbuf(g, half):
                    act.wait_ge(conv_done, count(2 * GROUPS, nxt, 2 * g + half + 1))
                    act.wait_ge(shuf_done, count(2 * QUADS, nxt, 2 * ((g - 3) // 2) + 2 if g >= 3 else 0))
                    if g == 2:
                        act.wait_ge(offT_done, count(1, nxt, 0))
                    nc.scalar.activation(conv_sb[:, g % 3, half * HALF:(half + 1) * HALF], pair_ps[half][:, :],
                                         ACT.Identity, bias=bias0[:, g:g + 1]).then_inc(conv_out, 1)

                def sums1_of(q):
                    act.wait_ge(x_loaded[u][q], (new - u) * 8 + 16)
                    if q == 0:
                        act.wait_ge(low1_done, count(2 * QUADS, new, 0))
                        act.wait_ge(mean1_done, count(1, new, 0))
                    for n, func in enumerate((ACT.Identity, ACT.Square)):
                        act.wait_ge(sums_done, count(2 * QUADS, new, 2 * q + n))
                        nc.scalar.activation(norm1[:, :], x_in[:, u, q, :], func,
                                             accum_out=sums1[:, n, q:q + 1]).then_inc(sums_done, 1)

                def apply1(q):
                    act.wait_ge(scale1_done, count(1, new, 1))
                    act.wait_ge(low1_done, count(2 * QUADS, new, 2 * q))
                    nc.scalar.activation(norm1[:, :], x_in[:, u, q, :], ACT.Identity, bias=gs1[:, 4, q:q + 1],
                                         scale=gs1[:, 3, q:q + 1]).then_inc(norm1_done, 1)
                    act.wait_ge(conv_done, count(2 * GROUPS, nxt, 4 * q + 4))
                    for e in (0, 1):
                        p = slice(64 * e, 64 * e + 64)
                        nc.scalar.activation(
                            plane(split1[p, 2 * q + e, :], 1, 1, HEIGHT),
                            x_in[p, u, q, :].rearrange("p (r c) -> p r c", c=WIDTH), ACT.Identity,
                            bias=gs1[p, 4, q:q + 1], scale=gs1[p, 3, q:q + 1]).then_inc(norm1_done, 1)

                def root2(q):
                    act.wait_ge(var2_done, count(QUADS, nxt, q + 1))
                    nc.scalar.activation(gs2[:, q, 2:3], gs2[:, q, 1:2], ACT.Sqrt, bias=eps_sb[:, 0:1])\
                      .then_inc(root2_done, 1)

                def scale_w1(q):
                    act.wait_ge(scale2_done, count(QUADS, nxt, q + 1))
                    act.wait_ge(in_done, count(2, nxt, 0))
                    w = slice(q * CH, (q + 1) * CH)
                    nc.scalar.activation(w1_norm[:, w], w1[:, w], ACT.Identity, scale=gs2[:, q, 3:4])\
                      .then_inc(w1_done, 1)

                def h_out():
                    act.wait_ge(bias_done, count(1, nxt, 1))
                    act.wait_ge(tile_done, count(TILES, nxt, 0))
                    act.wait_ge(h_low, count(1, nxt, 0))
                    act.wait_ge(diff_done, count(3, nxt, 0))
                    for half in (0, 1):
                        act.wait_ge(in_done, count(2, nxt, half + 1))
                        nc.scalar.activation(
                            plane(h_sb[:, :], 1 + half * HROWS, 1, HROWS),
                            pair_ps[half][:, :].rearrange("p (r c) -> p r c", c=WIDTH), ACT.Relu,
                            bias=h_bias[:, 0:1], scale=bn_s[:, 0:1]).then_inc(h_done, 1)
                    act.wait_ge(h_done, count(2, nxt, 2))
                    act.wait_ge(off_done, count(2, nxt, 0))
                    nc.scalar.activation(h_split[:, 0, :], h_sb[:, :], ACT.Copy).then_inc(h_high, 1)

                def tile_to_sbuf(m):
                    act.wait_ge(tile_done, count(TILES, nxt, m + 1))
                    act.wait_ge(tile_stored[m % TBUFS], count(16 * TILES // TBUFS, nxt, 16 * (m // TBUFS)))
                    nc.scalar.activation(table_sb[:, m % TBUFS, :], shuf_ps[:, :], ACT.Copy).then_inc(tile_out, 1)

                def offsets_out(image, half):
                    act.wait_ge(off_done, count(2, image, half + 1))
                    act.wait_ge(offT_done, count(1, image, 0))
                    nc.scalar.activation(offs_sb[:, half * HALF:(half + 1) * HALF], pair_ps[half][0:2 * OFFS, :],
                                         ACT.Identity, bias=bias_off[0:2 * OFFS, 0:1]).then_inc(off_out, 1)

                for s in range(CHUNKS):
                    image, c = chunk_at(s, 2)
                    if image is not None and c % TAPS == TAPS - 1:
                        deform_out(image, c // TAPS)
                    late = [unit for unit in UNITS[s - 1][1:] if unit[0] == "c"] if a2 and s else []
                    for unit in late:
                        conv_to_sbuf(*unit[1:])
                    for unit in UNITS[s][:1] if a2 else []:
                        if unit[0] == "c":
                            conv_to_sbuf(*unit[1:])
                    if b and s == 0:
                        offsets_out(t, 1)
                    if a2 and s in ROOT2:
                        root2(ROOT2.index(s))
                    if a2 and s in W1:
                        scale_w1(W1.index(s))
                    if a1 and s == 7:
                        act.wait_ge(var1_done, count(1, new, 1))
                        nc.scalar.activation(gs1[:, 2, :], gs1[:, 1, :], ACT.Sqrt, bias=eps_sb[:, 0:1])\
                          .then_inc(root1_done, 1)
                    image, c = chunk_at(s, 0)
                    if image is not None:
                        value_out(image, c)
                    if a2 and s == DIFF_SLOT:
                        h_out()
                    for m in TABLE_SLOTS.get(s, ()) if a2 else ():
                        tile_to_sbuf(m)
                        if m == 5:
                            offsets_out(nxt, 0)
                    if a1 and s in SUM_SLOTS:
                        sums1_of(SUM_SLOTS.index(s))
                    if a1 and s in APPLY_SLOTS:
                        apply1(APPLY_SLOTS.index(s))
                    for q in range(QUADS):
                        image, c = chunk_at(s, 2 + q)
                        if image is not None and c % TAPS == TAPS - 1:
                            relu_out(image, c // TAPS, q)

            run(act, step)

        @block.vector
        def _(dve):
            nc.vector.memset(bias0[:, :], 0.0)
            nc.vector.memset(bias_off[:, :], 0.0).then_inc(zeroed, 1)
            nc.vector.memset(split1[:, :, :].rearrange("p a b -> p (a b)").bitcast(f32), 0.0)
            nc.vector.memset(h_sb[:, :], 0.0)
            nc.vector.memset(eps_sb[:, :], EPS).then_inc(zeroed, 1)
            dve.wait_ge(bn_sqrt, 1)
            nc.vector.reciprocal(bn_t[:, :], bn_tmp[:, :]).then_inc(bn_chain, 1)
            dve.wait_ge(bn_chain, 1)
            nc.vector.tensor_tensor(bn_s[:, :], bn_t[:, :], bn_sb[:, :, 0], ALU.mult)
            nc.vector.tensor_tensor(bn_tmp[:, :], bn_sb[:, :, 4], bn_sb[:, :, 2], ALU.subtract).then_inc(bn_chain, 1)
            dve.wait_ge(bn_chain, 2)
            nc.vector.tensor_tensor(bn_t[:, :], bn_tmp[:, :], bn_s[:, :], ALU.mult).then_inc(bn_chain, 1)
            dve.wait_ge(bn_chain, 3)
            nc.vector.tensor_tensor(bn_t[:, :], bn_t[:, :], bn_sb[:, :, 1], ALU.add).then_inc(bn_chain, 1)
            dve.wait_ge(w_high, 1)
            for g in range(GROUPS):
                nc.vector.tensor_tensor(wg[:, g, :, GIN:2 * GIN], raw_wg[:, g * TAPS * GIN:(g + 1) * TAPS * GIN]
                                        .rearrange("p (k o) -> p k o", o=GIN), wg[:, g, :, 0:GIN], ALU.subtract)
            nc.vector.tensor_tensor(wo[:, :, OFFS:2 * OFFS], raw_wo.rearrange("p (k o) -> p k o", o=OFFS),
                                    wo[:, :, 0:OFFS], ALU.subtract).then_inc(w_low, 1)

            def step(t, u, tail, b, a2, a1):
                last, nxt, new = t - 1, t + 1, t + 2
                pn = (u + 1) % 2

                def chunk_at(s, lag):
                    v = s - SHIFT - lag
                    if v >= 0:
                        return (t, u, v) if b else (None, None, None)
                    return (last, pn, v + CHUNKS) if tail and v + CHUNKS >= 0 else (None, None, None)

                def interpolate(image, parity, c):
                    half, k = divmod(c, TAPS)
                    first = (c % RING) * PER
                    dve.wait_ge(gathered[c % RING],
                                count(16 * PER * CHUNKS // RING, image, 16 * PER * (c // RING + 1)))
                    for i in range(PER):
                        r = rows[:, first + i, :]
                        op = nc.vector.scalar_tensor_tensor(
                            r[:, 0:2 * CH], r[:, 2 * CH:4 * CH], frac[:, parity, half * PER + i, k, 0:1],
                            r[:, 0:2 * CH], ALU.mult, ALU.add)
                    op.then_inc(lerp_y, 1)
                    dve.wait_ge(valT_done, count(CHUNKS, image, c - 1))
                    dve.wait_ge(lerp_y, count(CHUNKS, image, c + 1))
                    for i in range(PER):
                        r = rows[:, first + i, :]
                        op = nc.vector.scalar_tensor_tensor(
                            val[:, c % 2, i * CH:(i + 1) * CH], r[:, CH:2 * CH],
                            frac[:, parity, half * PER + i, k, 1:2], r[:, 0:CH], ALU.mult, ALU.add)
                    op.then_inc(val_done, 1)

                def add_residual(image, parity, half, q):
                    dve.wait_ge(relu_done, count(2 * QUADS, image, half * QUADS + q + 1))
                    nc.vector.tensor_tensor(res[:, q, :], res[:, q, :],
                                            x_mid[:, parity, q, half * HALF:(half + 1) * HALF], ALU.add)\
                      .then_inc(sum_done, 1)

                def variance1():
                    dve.wait_ge(mean1_done, count(1, new, 1))
                    nc.vector.tensor_scalar(gs1[:, 0:2, :].rearrange("p a b -> p (a b)"), stat1_ps, 1.0 / PIX, None,
                                            ALU.mult).then_inc(read1_done, 1)
                    dve.wait_ge(read1_done, count(1, new, 1))
                    nc.vector.tensor_tensor(gs1[:, 5, :], gs1[:, 0, :], gs1[:, 0, :], ALU.mult).then_inc(chain1, 1)
                    dve.wait_ge(chain1, count(2, new, 1))
                    nc.vector.tensor_tensor(gs1[:, 1, :], gs1[:, 1, :], gs1[:, 5, :], ALU.subtract)\
                      .then_inc(var1_done, 1)

                def scale1():
                    dve.wait_ge(root1_done, count(1, new, 1))
                    nc.vector.reciprocal(gs1[:, 3, :], gs1[:, 2, :]).then_inc(chain1, 1)
                    dve.wait_ge(chain1, count(2, new, 2))
                    nc.vector.scalar_tensor_tensor(gs1[:, 4, :], gs1[:, 0, :], -1.0, gs1[:, 3, :], ALU.mult,
                                                   ALU.mult).then_inc(scale1_done, 1)

                def low1(q):
                    for e in (0, 1):
                        p, o = slice(64 * e, 64 * e + 64), slice(64 - 64 * e, 128 - 64 * e)
                        dve.wait_ge(norm1_done, count(3 * QUADS, new, 3 * q + e + 2))
                        nc.vector.tensor_tensor(
                            plane(split1[o, 2 * q + e, :], 1, 1, HEIGHT),
                            norm1[p, :].rearrange("p (r c) -> p r c", c=WIDTH),
                            plane(split1[p, 2 * q + e, :], 1, 1, HEIGHT), ALU.subtract).then_inc(low1_done, 1)

                def add_shuffled(q, half):
                    dve.wait_ge(shuf_done, count(2 * QUADS, nxt, 2 * q + half + 1))
                    dve.wait_ge(sum_done, count(2 * QUADS, last, half * QUADS + q + 1))
                    h = slice(half * HALF, (half + 1) * HALF)
                    nc.vector.tensor_tensor(x_mid[:, pn, q, h], shuf_ps[:, :], x_in[:, pn, q, h], ALU.add)\
                      .then_inc(mid_done, 1)

                def statistics2(q):
                    dve.wait_ge(mid_done, count(2 * QUADS, nxt, 2 * q + 2))
                    for a in (0, 1):
                        op = nc.vector.bn_stats(raw2[:, a, :], x_mid[:, pn, q, a * HALF:(a + 1) * HALF])
                    op.then_inc(agg2_chain, 1)
                    dve.wait_ge(agg2_chain, count(2 * QUADS, nxt, 2 * q + 1))
                    dve.sem_inc(dve_passed, 1)
                    nc.vector.bn_aggr(mv2[:, q, :], raw2[:, :, :]).then_inc(agg2_chain, 1)
                    dve.wait_ge(agg2_chain, count(2 * QUADS, nxt, 2 * q + 2))
                    nc.vector.scalar_tensor_tensor(mv2[:, q, 1:2], mv2[:, q, 0:1], mv2[:, q, 0:1], mv2[:, q, 1:2],
                                                   ALU.mult, ALU.add).then_inc(stats2_done, 1)

                def variance2(q):
                    dve.wait_ge(mean2_done, count(QUADS, nxt, q + 1))
                    nc.vector.tensor_copy(gs2[:, q, 0:2], stat2_ps[:, 2 * q:2 * q + 2]).then_inc(read2_done, 1)
                    dve.wait_ge(read2_done, count(QUADS, nxt, q + 1))
                    nc.vector.tensor_tensor(gs2[:, q, 5:6], gs2[:, q, 0:1], gs2[:, q, 0:1], ALU.mult)\
                      .then_inc(square2, 1)
                    dve.wait_ge(square2, count(QUADS, nxt, q + 1))
                    nc.vector.tensor_tensor(gs2[:, q, 1:2], gs2[:, q, 1:2], gs2[:, q, 5:6], ALU.subtract)\
                      .then_inc(var2_done, 1)

                def scale2(q):
                    dve.wait_ge(root2_done, count(QUADS, nxt, q + 1))
                    nc.vector.reciprocal(gs2[:, q, 3:4], gs2[:, q, 2:3]).then_inc(recip2, 1)
                    dve.wait_ge(recip2, count(QUADS, nxt, q + 1))
                    nc.vector.scalar_tensor_tensor(gs2[:, q, 4:5], gs2[:, q, 0:1], -1.0, gs2[:, q, 3:4], ALU.mult,
                                                   ALU.mult).then_inc(scale2_done, 1)

                def differences():
                    dve.wait_ge(h_high, count(1, nxt, 1))
                    nc.vector.tensor_tensor(h_split[:, 1, :], h_sb[:, :], h_split[:, 0, :], ALU.subtract)\
                      .then_inc(h_low, 1)
                    dve.wait_ge(tile_done, count(TILES, nxt, 0))
                    nc.vector.tensor_tensor(dx, h_sb[:, 1:NDX + 1], h_sb[:, 0:NDX], ALU.subtract)\
                      .then_inc(diff_done, 1)
                    nc.vector.tensor_tensor(dy, h_sb[:, PITCH:PITCH + ROWS], h_sb[:, 0:ROWS], ALU.subtract)\
                      .then_inc(diff_done, 1)
                    dve.wait_ge(diff_done, count(3, nxt, 1))
                    nc.vector.tensor_tensor(dxy, dx[:, PITCH:PITCH + ROWS], dx[:, 0:ROWS], ALU.subtract)\
                      .then_inc(diff_done, 1)

                def coordinates():
                    dve.wait_ge(offT_done, count(1, t, 1))
                    nc.vector.tensor_tensor(pos[:, :], offT_ps[:, :], grid_sb[:, :], ALU.add).then_inc(pos_chain, 1)
                    dve.wait_ge(pos_chain, count(8, t, 1))
                    nc.vector.tensor_scalar(pos[:, :], pos[:, :], -1.0, float(HEIGHT), ALU.max, ALU.min)\
                      .then_inc(pos_chain, 1)
                    dve.wait_ge(pos_chain, count(8, t, 2))
                    nc.vector.tensor_copy(posi[:, :], pos[:, :]).then_inc(pos_chain, 1)
                    dve.wait_ge(pos_chain, count(8, t, 3))
                    nc.vector.tensor_copy(posf[:, :], posi[:, :]).then_inc(pos_chain, 1)
                    dve.wait_ge(pos_chain, count(8, t, 4))
                    nc.vector.tensor_tensor(posg[:, :], posf[:, :], pos[:, :], ALU.is_gt).then_inc(pos_chain, 1)
                    dve.wait_ge(pos_chain, count(8, t, 5))
                    nc.vector.tensor_tensor(posf[:, :], posf[:, :], posg[:, :], ALU.subtract).then_inc(pos_chain, 1)
                    dve.wait_ge(pos_chain, count(8, t, 6))
                    nc.vector.tensor_scalar(posf[:, :], posf[:, :], float(HEIGHT - 1), None, ALU.min)\
                      .then_inc(pos_chain, 1)
                    dve.wait_ge(pos_chain, count(8, t, 7))
                    yx = posf[:, :].rearrange("p (a b c) -> p a b c", b=TAPS, c=2)
                    row = posg[:, 0:8 * TAPS].rearrange("p (a b) -> p a b", b=TAPS)
                    nc.vector.scalar_tensor_tensor(row, yx[:, :, :, 0], float(PITCH), yx[:, :, :, 1], ALU.mult,
                                                   ALU.add).then_inc(pos_chain, 1)
                    dve.wait_ge(pos_chain, count(8, t, 8))
                    nc.vector.tensor_scalar(ridx[:, u, :, :], row, float(PITCH + 1), None, ALU.add)
                    nc.vector.tensor_tensor(frac[:, u, :, :, :].rearrange("p a b c -> p (a b c)"), pos[:, :],
                                            posf[:, :], ALU.subtract).then_inc(pos_done, 1)

                for s in range(CHUNKS):
                    image, parity, c = chunk_at(s, 0)
                    if image is not None:
                        interpolate(image, parity, c)
                    if a2 and s in VAR2[:3]:
                        variance2(VAR2.index(s))
                    if a2 and s in SCALE2:
                        scale2(SCALE2.index(s))
                    if a1 and s == 7:
                        variance1()
                    if a1 and s == 8:
                        scale1()
                    if a1 and s - 1 in APPLY_SLOTS:
                        low1(APPLY_SLOTS.index(s - 1))
                    for q in range(QUADS):
                        image, parity, c = chunk_at(s, 3 + q)
                        if image is not None and c % TAPS == TAPS - 1:
                            add_residual(image, parity, c // TAPS, q)
                    for unit in UNITS[s] if a2 else []:
                        if unit[0] == "s":
                            add_shuffled(*unit[1:])
                            if unit[2] == 1:
                                statistics2(unit[1])
                    if b and s == 0:
                        coordinates()
                    if a2 and s == VAR2[3]:
                        variance2(3)
                    if a2 and s == SCALE2[3]:
                        dve.wait_ge(shift_done, count(1, nxt, 1))
                        nc.vector.tensor_scalar(h_bias[:, :], shift_ps, bn_s[:, 0:1], bn_t[:, 0:1], ALU.mult, ALU.add)\
                          .then_inc(bias_done, 1)
                    if a2 and s == DIFF_SLOT:
                        differences()

            run(dve, step)

        @block.tensor
        def _(pe):
            pe.wait_ge(w_low, 1)

            def step(t, u, tail, b, a2, a1):
                last, nxt, new = t - 1, t + 1, t + 2
                pn = (u + 1) % 2

                def chunk_at(s, lag):
                    v = s - SHIFT - lag
                    if v >= 0:
                        return (t, v) if b else (None, None)
                    return (last, v + CHUNKS) if tail and v + CHUNKS >= 0 else (None, None)

                def transpose_values(image, c):
                    pe.wait_ge(val_done, count(CHUNKS, image, c + 1))
                    pe.wait_ge(val_out, count(CHUNKS, image, c - 1))
                    for i in range(PER):
                        op = nc.tensor.transpose(valT_ps[c % 2][:, i * CH:(i + 1) * CH],
                                                 val[:, c % 2, i * CH:(i + 1) * CH], eye_sb[:, :])
                    op.then_inc(valT_done, 1)

                def deform(image, c):
                    half, k = divmod(c, TAPS)
                    pe.wait_ge(val_out, count(CHUNKS, image, c + 1))
                    if k == 0:
                        pe.wait_ge(d_out, count(2, image, half))
                    nc.tensor.matmul(def_ps[:, :], wd[:, k * CH:(k + 1) * CH], valT[:, c % 2, :], start=k == 0,
                                     stop=k == TAPS - 1).then_inc(def_done, 1)

                def out_conv(image, half, q):
                    if q == 0:
                        pe.wait_ge(d_out, count(2, image, half + 1))
                    pe.wait_ge(relu_done, count(2 * QUADS, image, half * QUADS + q))
                    nc.tensor.matmul(out_ps[:, :], w2[:, q * 128:(q + 1) * 128], mid[:, :], start=True, stop=True)\
                      .then_inc(out_done, 1)

                def mean1():
                    pe.wait_ge(sums_done, count(2 * QUADS, new, 2 * QUADS))
                    if a2:
                        pe.wait_ge(read2_done, count(QUADS, nxt, 1))
                    nc.tensor.matmul(stat1_ps, blocks_sb[:, :], sums1[:, :, :].rearrange("p a b -> p (a b)"),
                                     start=True, stop=True).then_inc(mean1_done, 1)

                def mean2(q):
                    pe.wait_ge(stats2_done, count(QUADS, nxt, q + 1))
                    if q == 0:
                        pe.wait_ge(pos_done, count(1, nxt, 0))
                    elif q == 1 and a1:
                        pe.wait_ge(read1_done, count(1, new, 1))
                    else:
                        pe.wait_ge(read2_done, count(QUADS, nxt, q))
                    nc.tensor.matmul(stat2_ps[:, 2 * q:2 * q + 2], blocks_sb[:, :], mv2[:, q, :], start=True,
                                     stop=True).then_inc(mean2_done, 1)

                def group_conv(g, half):
                    pe.wait_ge(low1_done, count(2 * QUADS, nxt, g + 1))
                    n = 2 * g + half
                    if n >= 2:
                        pe.wait_ge(conv_out, count(2 * GROUPS, nxt, n - 1))
                    else:
                        pe.wait_ge(off_out, count(2, nxt, half - 1))
                    for k in range(TAPS):
                        ky, kx = divmod(k, 3)
                        op = nc.tensor.matmul(pair_ps[half][:, :], wg[:, g, k, :],
                                              plane(split1[:, g, :], ky + half * HROWS, kx, HROWS),
                                              start=k == 0, stop=k == TAPS - 1)
                    op.then_inc(conv_done, 1)

                def shuffle(q, half):
                    pe.wait_ge(conv_out, count(2 * GROUPS, nxt, 4 * q + 4))
                    if q == half == 0:
                        pe.wait_ge(tile_out, count(TILES, nxt, 0))
                    else:
                        pe.wait_ge(mid_done, count(2 * QUADS, nxt, 2 * q + half))
                    for e in (0, 1):
                        for jj in range(COLS // 2):
                            j = half * (COLS // 2) + jj
                            op = nc.tensor.matmul(
                                shuf_ps[64 * e:64 * e + 64, jj * GIN:(jj + 1) * GIN],
                                conv_sb[:, (2 * q + e) % 3, j:j + COLS * (GIN - 1) + 1:COLS], fold_sb[:, :],
                                start=True, stop=True)
                    op.then_inc(shuf_done, 1)

                def in_conv(q):
                    pe.wait_ge(w1_done, count(QUADS, nxt, q + 1))
                    for half in (0, 1):
                        if q == 0:
                            pe.wait_ge(conv_out, count(2 * GROUPS, nxt, 2 * GROUPS - 1 + half))
                        op = nc.tensor.matmul(pair_ps[half][:, :], w1_norm[:, q * CH:(q + 1) * CH],
                                              x_mid[:, pn, q, half * HALF:(half + 1) * HALF], start=q == 0,
                                              stop=q == QUADS - 1)
                        if q == QUADS - 1:
                            op.then_inc(in_done, 1)

                def shift_product():
                    pe.wait_ge(scale2_done, count(QUADS, nxt, QUADS))
                    for q in range(QUADS):
                        op = nc.tensor.matmul(shift_ps, w1[:, q * CH:(q + 1) * CH], gs2[:, q, 4:5], start=q == 0,
                                              stop=q == QUADS - 1)
                    op.then_inc(shift_done, 1)

                def table_tile(m):
                    pe.wait_ge(tile_out, count(TILES, nxt, m))
                    if m == 0:
                        pe.wait_ge(mid_done, count(2 * QUADS, nxt, 2 * QUADS))
                        pe.wait_ge(diff_done, count(3, nxt, 3))
                    r = slice(m * 128, (m + 1) * 128)
                    for i, src in enumerate((h_sb[:, r], dx[:, r], dy[:, r], dxy[:, r])):
                        op = nc.tensor.transpose(shuf_ps[:, i * CH:(i + 1) * CH], src, eye_sb[:, :])
                    op.then_inc(tile_done, 1)

                def offset_conv(m):
                    for n in range(4 * m, 4 * m + 4):
                        half, r = divmod(n, 2 * TAPS)
                        k, part = divmod(r, 2)
                        ky, kx = divmod(k, 3)
                        if n == 0:
                            pe.wait_ge(h_high, count(1, nxt, 1))
                            pe.wait_ge(h_low, count(1, nxt, 1))
                        op = nc.tensor.matmul(pair_ps[half][0:2 * OFFS, :], wo[:, k, :],
                                              plane(h_split[:, part, :], ky + half * HROWS, kx, HROWS),
                                              start=r == 0, stop=r == 2 * TAPS - 1)
                        if r == 2 * TAPS - 1:
                            op.then_inc(off_done, 1)

                def transpose_offsets():
                    pe.wait_ge(off_out, count(2, t, 2))
                    for i in range(8):
                        op = nc.tensor.matmul(offT_ps[:, i * OFFS:(i + 1) * OFFS], offs_sb[:, i * 128:(i + 1) * 128],
                                              ofold_sb[:, :], start=True, stop=True)
                    op.then_inc(offT_done, 1)

                for s in range(CHUNKS):
                    units = UNITS[s] if a2 else []
                    for unit in units[:1]:
                        (group_conv if unit[0] == "c" else shuffle)(*unit[1:])
                    if b and s == 0:
                        transpose_offsets()
                    if a2 and s == 13:
                        shift_product()
                    if a2 and s in TABLE_SLOTS:
                        offset_conv(TABLE_SLOTS[s][0])
                        table_tile(TABLE_SLOTS[s][0])
                    image, c = chunk_at(s, 0)
                    if image is not None:
                        transpose_values(image, c)
                    if a2 and s in MEAN2[:3]:
                        mean2(MEAN2.index(s))
                    if a1 and s == 6:
                        mean1()
                    for q in range(QUADS):
                        image, c = chunk_at(s, 2 + q)
                        if image is not None and c % TAPS == TAPS - 1:
                            out_conv(image, c // TAPS, q)
                    for unit in units[1:]:
                        (group_conv if unit[0] == "c" else shuffle)(*unit[1:])
                    for q in IN_CONV.get(s, ()) if a2 else ():
                        in_conv(q)
                    if a2 and s == MEAN2[3]:
                        mean2(3)
                    for m in TABLE_SLOTS.get(s, ())[1:] if a2 else ():
                        offset_conv(m)
                        table_tile(m)
                    image, c = chunk_at(s, 1)
                    if image is not None:
                        deform(image, c)

            run(pe, step)


def constants():
    import numpy as np

    eye = np.eye(128, dtype=np.float32)
    fold = np.concatenate([np.eye(64, dtype=np.float32)] * 2)
    blocks = np.kron(np.eye(8, dtype=np.float32), np.full((16, 16), 1 / 16, np.float32))
    offset_fold = np.concatenate([np.eye(18, dtype=np.float32)] * 2)
    grid = np.zeros((128, 8, 9, 2), np.float32)
    for p in range(128):
        for i in range(8):
            for k in range(9):
                y, x = divmod(i * 128 + p, 32)
                grid[p, i, k] = (y + k // 3 - 1, x + k % 3 - 1)
    return eye, fold, blocks, offset_fold, grid.reshape(128, -1)


def kernel(x, L0_conv_W, L0_conv_b, L1_conv_conv1_w, L1_conv_conv1_b, L1_conv_bn1_g, L1_conv_bn1_b, L1_conv_bn1_m,
           L1_conv_bn1_v, L1_conv_off_w, L1_conv_off_b, L1_conv_dconv_w, L1_conv_dconv_b, L1_conv_bn2_g,
           L1_conv_bn2_b, L1_conv_bn2_m, L1_conv_bn2_v, L1_conv_conv2_w, L1_conv_conv2_b, L1_conv_bn3_g,
           L1_conv_bn3_b, L1_conv_bn3_m, L1_conv_bn3_v):
    import numpy as np
    import concourse.bacc as bacc
    from concourse.bass_utils import run_bass_kernel_spmd

    def wide(*vectors):
        return np.stack([np.asarray(v).reshape(-1, 128).T for v in vectors], axis=-1)

    eye, fold, blocks, offset_fold, grid = constants()
    bn = np.concatenate([
        wide(L1_conv_bn1_g, L1_conv_bn1_b, L1_conv_bn1_m, L1_conv_bn1_v, L1_conv_conv1_b),
        wide(L1_conv_bn2_g, L1_conv_bn2_b, L1_conv_bn2_m, L1_conv_bn2_v, L1_conv_dconv_b),
        wide(L1_conv_bn3_g, L1_conv_bn3_b, L1_conv_bn3_m, L1_conv_bn3_v, L1_conv_conv2_b)], axis=1)
    arrays = {
        "x": np.asarray(x).reshape(16, 4, 128, 1024),
        "w_group": np.asarray(L0_conv_W).reshape(8, 64, 64, 9).transpose(2, 0, 3, 1).reshape(64, -1),
        "b_group": np.asarray(L0_conv_b).T,
        "w_in": np.asarray(L1_conv_conv1_w).T.reshape(4, 128, 128).transpose(1, 0, 2).reshape(128, -1),
        "w_off": np.asarray(L1_conv_off_w).reshape(18, 128, 9).transpose(1, 2, 0).reshape(128, -1),
        "b_off": np.asarray(L1_conv_off_b).reshape(18, 1),
        "w_def": np.asarray(L1_conv_dconv_w).reshape(128, 128, 9).transpose(1, 2, 0).reshape(128, -1),
        "w_out": np.asarray(L1_conv_conv2_w).T,
        "bn": bn, "eye": eye, "fold": fold, "blocks": blocks, "offset_fold": offset_fold, "grid": grid,
    }
    arrays = {name: np.ascontiguousarray(a) for name, a in arrays.items()}
    nc = bacc.Bacc("TRN2", target_bir_lowering=False, num_devices=1)
    args = [nc.dram_tensor(name, a.shape, mybir.dt.from_np(a.dtype), kind="ExternalInput").ap()
            for name, a in arrays.items()]
    tables = [nc.dram_tensor(f"table{n}", (9 * 128, 512), mybir.dt.float32, kind="Internal").ap() for n in (0, 1)]
    out = nc.dram_tensor("out", (16, 4, 128, 1024), mybir.dt.float32, kind="ExternalOutput").ap()
    build_program(nc, *args, tables, out)
    r = run_bass_kernel_spmd(nc, [arrays], core_ids=[0])
    return r.results[0]["out"].reshape(16, 512, 32, 32)
```

```python
import concourse.bass as bass
from concourse import mybir
from contextlib import ExitStack


def build_program(nc, x, w_group, b_group, w_in, w_off, b_off, w_def, w_out, bn, eye, fold, blocks, offset_fold,
                  grid, tables, out):
    f32, f16, i32, u32 = mybir.dt.float32, mybir.dt.float16, mybir.dt.int32, mybir.dt.uint32
    ALU = mybir.AluOpType
    ACT = mybir.ActivationFunctionType

    IMAGES, CHANNELS, HEIGHT, WIDTH = 16, 512, 32, 32
    PIX = HEIGHT * WIDTH
    HALF = PIX // 2
    HROWS = HEIGHT // 2
    QUADS = CHANNELS // 128
    GROUPS = 8
    GIN = CHANNELS // GROUPS
    TAPS = 9
    PITCH = WIDTH + 2
    PLANE = PITCH * (HEIGHT + 2)
    TILES = 9
    ROWS = TILES * 128
    HPLANE = PITCH * (HEIGHT + 3)
    NDX = ROWS + PITCH
    CH = 128
    OFFS = 2 * TAPS
    CHUNKS = 2 * TAPS
    SLOTS = CHUNKS
    SHIFT = 7
    RING = 3
    TBUFS = 3
    PER = 4
    ROW = 4 * CH
    COLS = PIX // GIN
    XBUFS = 4
    EPS = 1e-5

    ctx = ExitStack()
    with ctx:
        def sb(name, shape, dt):
            return ctx.enter_context(nc.sbuf_tensor("sb_" + name, shape, dt))

        def sem(name):
            return ctx.enter_context(nc.semaphore(name))

        xs = sb("xs", [128, XBUFS, QUADS, PIX], f32)
        split1 = sb("split1", [128, GROUPS, PLANE], f16)
        wg = sb("wg", [128, GROUPS, TAPS, 2 * GIN], f16)
        conv_sb = sb("conv_sb", [128, 3, PIX], f32)
        norm1 = sb("norm1", [128, PIX], f32)
        diff = sb("diff", [128, NDX + 2 * ROWS], f32)
        h_sb = sb("h_sb", [128, HPLANE], f32)
        h_split = sb("h_split", [128, 2, HPLANE], f16)
        table_sb = sb("table_sb", [128, TBUFS, ROW], f32)
        rows = sb("rows", [128, RING * PER, ROW], f32)
        val = sb("val", [128, 2, PER * CH], f32)
        valT = sb("valT", [128, 2, HALF], f32)
        w1 = sb("w1", [128, QUADS * CH], f32)
        w1_norm = sb("w1_norm", [128, QUADS * CH], f32)
        wo = sb("wo", [128, TAPS, 64], f16)
        wd = sb("wd", [128, TAPS * CH], f32)
        w2 = sb("w2", [128, QUADS * 128], f32)
        mid = sb("mid", [128, HALF], f32)
        res = sb("res", [128, QUADS, HALF], f32)
        eye_sb = sb("eye_sb", [128, 128], f32)
        blocks_sb = sb("blocks_sb", [128, 128], f32)
        fold_sb = sb("fold_sb", [128, GIN], f32)
        ofold_sb = sb("ofold_sb", [128, 2 * OFFS], f32)
        grid_sb = sb("grid_sb", [128, 8 * OFFS], f32)
        bias0 = sb("bias0", [128, GROUPS], f32)
        bias_off = sb("bias_off", [128, 1], f32)
        eps_sb = sb("eps_sb", [128, 1], f32)
        bn_sb = sb("bn_sb", [128, 6, 5], f32)
        bn_s = sb("bn_s", [128, 6], f32)
        bn_t = sb("bn_t", [128, 6], f32)
        bn_tmp = sb("bn_tmp", [128, 6], f32)
        raw2 = sb("raw2", [128, 2, 6], f32)
        sums1 = sb("sums1", [128, 2, QUADS], f32)
        mv2 = sb("mv2", [128, QUADS, 2], f32)
        gs1 = sb("gs1", [128, 6, QUADS], f32)
        gs2 = sb("gs2", [128, 6, QUADS], f32)
        h_bias = sb("h_bias", [128, 1], f32)
        pos = sb("pos", [128, 8 * OFFS], f32)
        posi = sb("posi", [128, 8 * OFFS], i32)
        posf = sb("posf", [128, 8 * OFFS], f32)
        posg = sb("posg", [128, 8 * OFFS], f32)
        frac = sb("frac", [128, 2, 8, TAPS, 2], f32)
        ridx = sb("ridx", [128, 2, 8, TAPS], i32)

        dx, dy, dxy = diff[:, 0:NDX], diff[:, NDX:NDX + ROWS], diff[:, NDX + ROWS:NDX + 2 * ROWS]
        offs_sb = w1_norm
        raw_wg = rows[:, :, :].rearrange("p a b -> p (a b)")[:, 0:GROUPS * TAPS * GIN]
        raw_wo = diff[:, 0:TAPS * OFFS]

        banks = [ctx.enter_context(nc.psum_tensor(f"bank{n}", [128, 512], f32)) for n in range(8)]
        pair_ps = banks[0:2]
        shuf_ps = banks[2]
        small_ps = banks[3]
        stat1_ps = small_ps[:, 0:2 * QUADS]
        stat2_ps = small_ps[:, 2 * QUADS:4 * QUADS]
        shift_ps = small_ps[:, 32:33]
        offT_ps = small_ps[:, 64:64 + 8 * OFFS]
        valT_ps = banks[4:6]
        def_ps = banks[6]
        out_ps = banks[7]

        weights_in = sem("weights_in")
        consts_in = sem("consts_in")
        pool_passed = sem("pool_passed")
        dve_passed = sem("dve_passed")
        zeroed = sem("zeroed")
        w_high = sem("w_high")
        w_rounded = sem("w_rounded")
        w_low = sem("w_low")
        bn_chain = sem("bn_chain")
        bn_sqrt = sem("bn_sqrt")
        x_loaded = [[sem(f"x_loaded{p}{q}") for q in range(QUADS)] for p in (0, 1)]
        sums_done = sem("sums_done")
        mean1_done = sem("mean1_done")
        read1_done = sem("read1_done")
        chain1 = sem("chain1")
        var1_done = sem("var1_done")
        root1_done = sem("root1_done")
        scale1_done = sem("scale1_done")
        norm1_done = sem("norm1_done")
        low1_done = sem("low1_done")
        stats2_done = sem("stats2_done")
        agg2_chain = sem("agg2_chain")
        mean2_done = sem("mean2_done")
        read2_done = sem("read2_done")
        square2 = sem("square2")
        recip2 = sem("recip2")
        var2_done = sem("var2_done")
        root2_done = sem("root2_done")
        scale2_done = sem("scale2_done")
        w1_done = sem("w1_done")
        shift_done = sem("shift_done")
        bias_done = sem("bias_done")
        conv_done = sem("conv_done")
        conv_out = sem("conv_out")
        shuf_done = sem("shuf_done")
        mid_done = sem("mid_done")
        in_done = sem("in_done")
        h_done = sem("h_done")
        h_high = sem("h_high")
        h_low = sem("h_low")
        diff_done = sem("diff_done")
        tile_done = sem("tile_done")
        tile_out = sem("tile_out")
        tile_stored = [sem(f"tile_stored{n}") for n in range(TBUFS)]
        off_done = sem("off_done")
        off_out = sem("off_out")
        offT_done = sem("offT_done")
        pos_chain = sem("pos_chain")
        pos_done = sem("pos_done")
        gathered = [sem(f"gathered{n}") for n in range(RING)]
        lerp_y = sem("lerp_y")
        val_done = sem("val_done")
        valT_done = sem("valT_done")
        val_out = sem("val_out")
        def_done = sem("def_done")
        d_out = sem("d_out")
        out_done = sem("out_done")
        relu_done = sem("relu_done")
        sum_done = sem("sum_done")
        stored = [sem(f"stored{n}") for n in range(QUADS)]

        N_CONSTS = 12
        POOL_GROUPS = 5

        def count(per, image, n):
            total = image * per + n
            return max(total, 0) if isinstance(image, int) else total

        def run(eng, step):
            for t in (-2, -1, 0, 1):
                step(t, t % XBUFS, t >= 1, t >= 0, t >= -1, True)
            with eng.Fori(0, (IMAGES - 4) // XBUFS) as j:
                for k in range(2, 2 + XBUFS):
                    step(XBUFS * j + k, k % XBUFS, True, True, True, True)
            step(IMAGES - 2, (IMAGES - 2) % XBUFS, True, True, True, False)
            step(IMAGES - 1, (IMAGES - 1) % XBUFS, True, True, False, False)
            step(IMAGES, IMAGES % XBUFS, True, False, False, False)

        CONV_FIRST = {3: (3, 1), 4: (4, 0), 5: (4, 1), 6: (5, 0), 7: (5, 1), 8: (6, 1), 9: (7, 0),
                      12: (0, 1), 13: (1, 1)}
        CONV_THEN = {2: (3, 0), 7: (6, 0), 9: (7, 1), 11: (0, 0), 12: (1, 0), 16: (2, 0), 17: (2, 1)}
        NEXT_CONV = 11
        OUT_LATE = (6, 9)
        SHUFFLE = {5: (1, 0), 6: (1, 1), 8: (2, 0), 9: (2, 1), 10: (3, 0), 11: (3, 1), 15: (0, 0), 16: (0, 1)}
        NEXT_SHUFFLE = 12
        STATS = {2: 0, 7: 1, 10: 2, 12: 3}
        PARTS2 = (slice(0, 3), slice(3, 4))
        MEAN2, VAR2, ROOT2, SCALE2 = (11, 13), (11, 13), (11, 13), (12, 14)
        W1 = {13: (0, 1, 2), 14: (3,)}
        IN_CONV = {14: (0, 1), 15: (2, 3)}
        SHIFT_SLOT = 15
        H_SLOT = 16
        OFFSET = {17: 0, 0: 1, 1: 2, 2: 3}
        TABLE = {0: (1, 3), 1: (1, 3), 2: (0, 1, 3), 3: (1, 3)}
        TRANSPOSE_OFFSETS, COORDINATES = 3, 4
        SUMS = {0: 0, 2: 1, 4: 2, 5: 3}
        MEAN1, VAR1, ROOT1, SCALE1 = 6, 8, 8, 9
        APPLY = {9: 0, 11: 1, 13: 2, 15: 3}

        def tile_at(s, place):
            if place not in TABLE.get(s, ()):
                return None
            return sum(len(TABLE[r]) for r in TABLE if r < s) + TABLE[s].index(place)

        def plane(ap, row, col, nrows):
            v = ap[:, row * PITCH:(row + nrows) * PITCH]
            return v.rearrange("p (r c) -> p r c", c=PITCH)[:, :, col:col + WIDTH]

        def chunk_at(s, lag, t, tail, b):
            v = s - SHIFT - lag
            if v >= 0:
                return (t, 0, v) if b else (None, 0, 0)
            return (t - 1, 1, v + CHUNKS) if tail and v + CHUNKS >= 0 else (None, 0, 0)

        def outputs_at(s, lag, t, tail, b):
            for q in range(QUADS):
                image, back, c = chunk_at(s, lag + q, t, tail, b)
                if image is not None and c % TAPS == TAPS - 1:
                    yield image, back, c // TAPS, q

        block = ctx.enter_context(nc.Block())

        @block.sync
        def _(sp):
            def load_constants():
                sp.wait_ge(zeroed, 1)
                for dst, src in ((blocks_sb[:, :], blocks), (bias0[0:64, :], b_group), (bn_sb[:, :, :], bn),
                                 (fold_sb[:, :], fold), (w1[:, :], w_in), (bias_off[0:OFFS, :], b_off),
                                 (bias_off[64:64 + OFFS, :], b_off), (eye_sb[:, :], eye),
                                 (ofold_sb[:, :], offset_fold), (grid_sb[:, :], grid), (wd[:, :], w_def),
                                 (w2[:, :], w_out)):
                    sp.dma_start(dst, src).then_inc(consts_in, 16)

            def step(t, u, tail, b, a2, a1):
                new = t + 2
                if a1:
                    sp.wait_ge(sum_done, count(2 * QUADS, t - 2, 2 * QUADS))
                    sp.wait_ge(sums_done, count(2 * QUADS, t, 2 * QUADS))
                    for q in range(QUADS):
                        sp.dma_start(xs[:, (u + 2) % XBUFS, q, :], x[bass.ds(new, 1), q].rearrange("a p n -> (a p) n"))\
                          .then_inc(x_loaded[u % 2][q], 16)
                if a1 and not a2:
                    load_constants()
                for s in range(SLOTS):
                    for m in [tile_at(s, place) for place in TABLE.get(s, ())] if b else ():
                        sp.wait_ge(tile_out, count(TILES, t, m + 1))
                        sp.dma_start(tables[u % 2][m * 128:(m + 1) * 128, :], table_sb[:, m % TBUFS, :])\
                          .then_inc(tile_stored[m % TBUFS], 16)
                    for image, _, half, q in outputs_at(s, 5, t, tail, b):
                        sp.wait_ge(sum_done, count(2 * QUADS, image, half * QUADS + q + 1))
                        dst = out[bass.ds(image, 1), q].rearrange("a p n -> (a p) n")
                        sp.dma_start(dst[:, half * HALF:(half + 1) * HALF], res[:, q, :]).then_inc(stored[q], 16)

            run(sp, step)
            for q in range(QUADS):
                sp.wait_ge(stored[q], 16 * IMAGES * 2)

        @block.gpsimd
        def _(pool):
            def step(t, u, tail, b, a2, a1):
                if not b:
                    return
                pool.wait_ge(pos_done, count(1, t, 1))
                for n in range(TBUFS):
                    pool.wait_ge(tile_stored[n], count(16 * TILES // TBUFS, t, 16 * TILES // TBUFS))
                for c in range(CHUNKS):
                    half, k = divmod(c, TAPS)
                    pool.wait_ge(val_done, count(CHUNKS, t, c - RING + 1))
                    pool.sem_inc(pool_passed, 1)
                    for i in range(PER):
                        pool.indirect_dma_start(
                            out=rows[:, (c % RING) * PER + i, :], out_offset=None, in_=tables[u % 2],
                            in_offset=bass.IndirectOffsetOnAxis(
                                ap=ridx[:, u % 2, half * PER + i, k:k + 1].bitcast(u32), axis=0),
                        ).then_inc(gathered[c % RING], 16)

            pool.wait_ge(weights_in, 3 * 16)
            for g in range(POOL_GROUPS, GROUPS):
                nc.gpsimd.tensor_copy(wg[:, g, :, 0:GIN], raw_wg[:, g * TAPS * GIN:(g + 1) * TAPS * GIN]
                                      .rearrange("p (k o) -> p k o", o=GIN)).then_inc(w_high, 1)

            run(pool, step)

        @block.scalar
        def _(act):
            for dst, src in ((raw_wg[0:64, :], w_group), (raw_wg[64:128, :], w_group), (raw_wo, w_off)):
                act.dma_start(dst, src).then_inc(weights_in, 16)

            def batch_norms():
                act.wait_ge(consts_in, 16 * N_CONSTS)
                act.wait_ge(zeroed, 2)
                nc.scalar.activation(bn_tmp[:, :], bn_sb[:, :, 3], ACT.Sqrt, bias=eps_sb[:, 0:1]).then_inc(bn_sqrt, 1)
                act.wait_ge(bn_chain, 4)

            def value_out(image, c):
                act.wait_ge(valT_done, count(CHUNKS, image, c + 1))
                act.wait_ge(def_done, count(CHUNKS, image, c - 1))
                nc.scalar.activation(valT[:, c % 2, :], valT_ps[c % 2][:, :], ACT.Copy).then_inc(val_out, 1)

            def deform_out(image, half):
                act.wait_ge(def_done, count(CHUNKS, image, TAPS * (half + 1)))
                act.wait_ge(out_done, count(2 * QUADS, image, half * QUADS))
                nc.scalar.activation(mid[:, :], def_ps[:, :], ACT.Identity, bias=bn_t[:, 1:2],
                                     scale=bn_s[:, 1:2]).then_inc(d_out, 1)

            def relu_out(image, half, q):
                act.wait_ge(out_done, count(2 * QUADS, image, half * QUADS + q + 1))
                act.wait_ge(stored[q], count(32, image, 16 * half))
                nc.scalar.activation(res[:, q, :], out_ps[:, :], ACT.Relu, bias=bn_t[:, 2 + q:3 + q],
                                     scale=bn_s[:, 2 + q:3 + q]).then_inc(relu_done, 1)

            def conv_to_sbuf(image, g, half):
                act.wait_ge(conv_done, count(2 * GROUPS, image, 2 * g + half + 1))
                act.wait_ge(shuf_done, count(2 * QUADS, image, 2 * ((g - 3) // 2) + 2 if g >= 3 else 0))
                nc.scalar.activation(conv_sb[:, g % 3, half * HALF:(half + 1) * HALF], pair_ps[half][:, :],
                                     ACT.Identity, bias=bias0[:, g:g + 1]).then_inc(conv_out, 1)

            def step(t, u, tail, b, a2, a1):
                nxt, new = t + 1, t + 2
                un = (u + 2) % XBUFS

                def sum1(q, n):
                    act.wait_ge(x_loaded[u % 2][q], (new - u % 2) * 8 + 16)
                    if q == n == 0:
                        act.wait_ge(low1_done, count(2 * QUADS, new, 0))
                        act.wait_ge(mean1_done, count(1, new, 0))
                    act.wait_ge(sums_done, count(2 * QUADS, new, 2 * q + n))
                    nc.scalar.activation(norm1[:, :], xs[:, un, q, :], (ACT.Identity, ACT.Square)[n],
                                         accum_out=sums1[:, n, q:q + 1]).then_inc(sums_done, 1)

                def apply1(q):
                    act.wait_ge(scale1_done, count(1, new, 1))
                    act.wait_ge(low1_done, count(2 * QUADS, new, 2 * q))
                    nc.scalar.activation(norm1[:, :], xs[:, un, q, :], ACT.Identity, bias=gs1[:, 4, q:q + 1],
                                         scale=gs1[:, 3, q:q + 1]).then_inc(norm1_done, 1)

                def high1(q, e):
                    act.wait_ge(conv_done, count(2 * GROUPS, nxt, 4 * q + 4))
                    p = slice(64 * e, 64 * e + 64)
                    nc.scalar.activation(
                        plane(split1[p, 2 * q + e, :], 1, 1, HEIGHT),
                        xs[p, un, q, :].rearrange("p (r c) -> p r c", c=WIDTH), ACT.Identity,
                        bias=gs1[p, 4, q:q + 1], scale=gs1[p, 3, q:q + 1]).then_inc(norm1_done, 1)

                def root2(part):
                    quads = PARTS2[part]
                    act.wait_ge(var2_done, count(2, nxt, part + 1))
                    nc.scalar.activation(gs2[:, 2, quads], gs2[:, 1, quads], ACT.Sqrt, bias=eps_sb[:, 0:1])\
                      .then_inc(root2_done, 1)

                def scale_w1(q):
                    act.wait_ge(scale2_done, count(2, nxt, 1 + q // 3))
                    act.wait_ge(in_done, count(2, nxt, 0))
                    act.wait_ge(offT_done, count(1, t, 1))
                    w = slice(q * CH, (q + 1) * CH)
                    nc.scalar.activation(w1_norm[:, w], w1[:, w], ACT.Identity, scale=gs2[:, 3, q:q + 1])\
                      .then_inc(w1_done, 1)

                def h_out():
                    act.wait_ge(bias_done, count(1, nxt, 1))
                    act.wait_ge(tile_done, count(TILES, nxt, 0))
                    act.wait_ge(h_low, count(1, nxt, 0))
                    act.wait_ge(diff_done, count(3, nxt, 0))
                    for half in (0, 1):
                        act.wait_ge(in_done, count(2, nxt, half + 1))
                        nc.scalar.activation(
                            plane(h_sb[:, :], 1 + half * HROWS, 1, HROWS),
                            pair_ps[half][:, :].rearrange("p (r c) -> p r c", c=WIDTH), ACT.Relu,
                            bias=h_bias[:, 0:1], scale=bn_s[:, 0:1]).then_inc(h_done, 1)
                    act.wait_ge(h_done, count(2, nxt, 2))
                    act.wait_ge(off_done, count(1, nxt, 0))
                    nc.scalar.activation(h_split[:, 0, :], h_sb[:, :], ACT.Copy).then_inc(h_high, 1)

                def tile_to_sbuf(m):
                    act.wait_ge(tile_done, count(TILES, t, m + 1))
                    act.wait_ge(tile_stored[m % TBUFS], count(16 * TILES // TBUFS, t, 16 * (m // TBUFS)))
                    nc.scalar.activation(table_sb[:, m % TBUFS, :], shuf_ps[:, :], ACT.Copy).then_inc(tile_out, 1)

                def offsets_out():
                    act.wait_ge(off_done, count(1, t, 1))
                    act.wait_ge(in_done, count(2, t, 2))
                    nc.scalar.activation(offs_sb[:, :], small_ps[:, :], ACT.Identity, bias=bias_off[:, 0:1])\
                      .then_inc(off_out, 1)

                for s in range(SLOTS):
                    if s == 0 and a2:
                        conv_to_sbuf(nxt, *CONV_THEN[SLOTS - 1])
                    if s - 1 in CONV_THEN and (a1 if s > NEXT_CONV else a2):
                        conv_to_sbuf(new if s > NEXT_CONV else nxt, *CONV_THEN[s - 1])
                    if a2 and s == H_SLOT:
                        h_out()
                    image, _, c = chunk_at(s, 3, t, tail, b)
                    if image is not None and c % TAPS == TAPS - 1:
                        deform_out(image, c // TAPS)
                    if a1 and not a2 and s == MEAN1:
                        batch_norms()
                    if b and s == TRANSPOSE_OFFSETS:
                        offsets_out()
                    if a1 and s == ROOT1:
                        act.wait_ge(var1_done, count(1, new, 1))
                        nc.scalar.activation(gs1[:, 2, :], gs1[:, 1, :], ACT.Sqrt, bias=eps_sb[:, 0:1])\
                          .then_inc(root1_done, 1)
                    if b and tile_at(s, 0) is not None:
                        tile_to_sbuf(tile_at(s, 0))
                    if a1 and s in SUMS:
                        sum1(SUMS[s], 0)
                    if s in CONV_FIRST and s not in OUT_LATE and (a1 if s >= NEXT_CONV else a2):
                        conv_to_sbuf(new if s >= NEXT_CONV else nxt, *CONV_FIRST[s])
                    image, _, c = chunk_at(s, 1, t, tail, b)
                    if image is not None:
                        value_out(image, c)
                    for q in W1.get(s, ()) if a2 else ():
                        scale_w1(q)
                    if a2 and s in ROOT2:
                        root2(ROOT2.index(s))
                    for image, _, half, q in outputs_at(s, 4, t, tail, b):
                        relu_out(image, half, q)
                    if b and tile_at(s, 1) is not None:
                        tile_to_sbuf(tile_at(s, 1))
                    if a1 and s in APPLY:
                        apply1(APPLY[s])
                        high1(APPLY[s], 0)
                    if s in OUT_LATE and a2:
                        conv_to_sbuf(nxt, *CONV_FIRST[s])
                    if a1 and s in SUMS:
                        sum1(SUMS[s], 1)
                    if a1 and s in APPLY:
                        high1(APPLY[s], 1)
                    if b and tile_at(s, 3) is not None:
                        tile_to_sbuf(tile_at(s, 3))

            run(act, step)

        @block.vector
        def _(dve):
            nc.vector.memset(bias0[:, :], 0.0)
            nc.vector.memset(bias_off[:, :], 0.0).then_inc(zeroed, 1)
            nc.vector.memset(split1[:, :, :].rearrange("p a b -> p (a b)").bitcast(f32), 0.0)
            nc.vector.memset(wo[:, :, :].rearrange("p a b -> p (a b)").bitcast(f32), 0.0)
            nc.vector.memset(h_sb[:, :], 0.0)
            nc.vector.memset(eps_sb[:, :], EPS).then_inc(zeroed, 1)
            dve.wait_ge(weights_in, 3 * 16)
            for g in range(POOL_GROUPS):
                nc.vector.tensor_copy(wg[:, g, :, 0:GIN], raw_wg[:, g * TAPS * GIN:(g + 1) * TAPS * GIN]
                                      .rearrange("p (k o) -> p k o", o=GIN))
            dve.wait_ge(zeroed, 2)
            nc.vector.tensor_copy(wo[:, :, 0:OFFS], raw_wo.rearrange("p (k o) -> p k o", o=OFFS))\
              .then_inc(w_rounded, 1)
            dve.wait_ge(w_rounded, 1)
            for g in range(GROUPS):
                if g >= POOL_GROUPS:
                    dve.wait_ge(w_high, g - POOL_GROUPS + 1)
                nc.vector.tensor_tensor(wg[:, g, :, GIN:2 * GIN], raw_wg[:, g * TAPS * GIN:(g + 1) * TAPS * GIN]
                                        .rearrange("p (k o) -> p k o", o=GIN), wg[:, g, :, 0:GIN], ALU.subtract)
            nc.vector.tensor_tensor(wo[:, :, OFFS:2 * OFFS], raw_wo.rearrange("p (k o) -> p k o", o=OFFS),
                                    wo[:, :, 0:OFFS], ALU.subtract).then_inc(w_low, 1)
            dve.wait_ge(bn_sqrt, 1)
            nc.vector.reciprocal(bn_t[:, :], bn_tmp[:, :]).then_inc(bn_chain, 1)
            dve.wait_ge(bn_chain, 1)
            nc.vector.tensor_tensor(bn_s[:, :], bn_t[:, :], bn_sb[:, :, 0], ALU.mult)
            nc.vector.tensor_tensor(bn_tmp[:, :], bn_sb[:, :, 4], bn_sb[:, :, 2], ALU.subtract).then_inc(bn_chain, 1)
            dve.wait_ge(bn_chain, 2)
            nc.vector.tensor_tensor(bn_t[:, :], bn_tmp[:, :], bn_s[:, :], ALU.mult).then_inc(bn_chain, 1)
            dve.wait_ge(bn_chain, 3)
            nc.vector.tensor_tensor(bn_t[:, :], bn_t[:, :], bn_sb[:, :, 1], ALU.add).then_inc(bn_chain, 1)

            def step(t, u, tail, b, a2, a1):
                nxt, new = t + 1, t + 2

                def interpolate(image, parity, c):
                    half, k = divmod(c, TAPS)
                    first = (c % RING) * PER
                    dve.wait_ge(gathered[c % RING],
                                count(16 * PER * CHUNKS // RING, image, 16 * PER * (c // RING + 1)))
                    for i in range(PER):
                        r = rows[:, first + i, :]
                        op = nc.vector.scalar_tensor_tensor(
                            r[:, 0:2 * CH], r[:, 2 * CH:4 * CH], frac[:, parity, half * PER + i, k, 0:1],
                            r[:, 0:2 * CH], ALU.mult, ALU.add)
                    op.then_inc(lerp_y, 1)
                    dve.wait_ge(valT_done, count(CHUNKS, image, c - 1))
                    dve.wait_ge(lerp_y, count(CHUNKS, image, c + 1))
                    for i in range(PER):
                        r = rows[:, first + i, :]
                        op = nc.vector.scalar_tensor_tensor(
                            val[:, c % 2, i * CH:(i + 1) * CH], r[:, CH:2 * CH],
                            frac[:, parity, half * PER + i, k, 1:2], r[:, 0:CH], ALU.mult, ALU.add)
                    op.then_inc(val_done, 1)

                def add_residual(image, buf, half, q):
                    dve.wait_ge(relu_done, count(2 * QUADS, image, half * QUADS + q + 1))
                    nc.vector.tensor_tensor(res[:, q, :], res[:, q, :],
                                            xs[:, buf, q, half * HALF:(half + 1) * HALF], ALU.add)\
                      .then_inc(sum_done, 1)

                def variance1():
                    dve.wait_ge(mean1_done, count(1, new, 1))
                    nc.vector.tensor_scalar(gs1[:, 0:2, :].rearrange("p a b -> p (a b)"), stat1_ps, 1.0 / PIX, None,
                                            ALU.mult).then_inc(read1_done, 1)
                    dve.wait_ge(read1_done, count(1, new, 1))
                    nc.vector.tensor_tensor(gs1[:, 5, :], gs1[:, 0, :], gs1[:, 0, :], ALU.mult).then_inc(chain1, 1)
                    dve.wait_ge(chain1, count(2, new, 1))
                    nc.vector.tensor_tensor(gs1[:, 1, :], gs1[:, 1, :], gs1[:, 5, :], ALU.subtract)\
                      .then_inc(var1_done, 1)

                def scale1():
                    dve.wait_ge(root1_done, count(1, new, 1))
                    nc.vector.reciprocal(gs1[:, 3, :], gs1[:, 2, :]).then_inc(chain1, 1)
                    dve.wait_ge(chain1, count(2, new, 2))
                    nc.vector.scalar_tensor_tensor(gs1[:, 4, :], gs1[:, 0, :], -1.0, gs1[:, 3, :], ALU.mult,
                                                   ALU.mult).then_inc(scale1_done, 1)

                def low1(q):
                    for e in (0, 1):
                        p, o = slice(64 * e, 64 * e + 64), slice(64 - 64 * e, 128 - 64 * e)
                        dve.wait_ge(norm1_done, count(3 * QUADS, new, 3 * q + e + 2))
                        nc.vector.tensor_tensor(
                            plane(split1[o, 2 * q + e, :], 1, 1, HEIGHT),
                            norm1[p, :].rearrange("p (r c) -> p r c", c=WIDTH),
                            plane(split1[p, 2 * q + e, :], 1, 1, HEIGHT), ALU.subtract).then_inc(low1_done, 1)

                def add_shuffled(image, buf, q, half):
                    dve.wait_ge(shuf_done, count(2 * QUADS, image, 2 * q + half + 1))
                    h = slice(half * HALF, (half + 1) * HALF)
                    nc.vector.tensor_tensor(xs[:, buf, q, h], shuf_ps[:, :], xs[:, buf, q, h], ALU.add)\
                      .then_inc(mid_done, 1)

                def statistics2(q):
                    dve.wait_ge(mid_done, count(2 * QUADS, nxt, 2 * q + 2))
                    for a in (0, 1):
                        op = nc.vector.bn_stats(raw2[:, a, :], xs[:, (u + 1) % XBUFS, q, a * HALF:(a + 1) * HALF])
                    op.then_inc(agg2_chain, 1)
                    dve.wait_ge(agg2_chain, count(2 * QUADS, nxt, 2 * q + 1))
                    dve.wait_ge(mean2_done, count(2, nxt, 0))
                    dve.sem_inc(dve_passed, 1)
                    nc.vector.bn_aggr(mv2[:, q, :], raw2[:, :, :]).then_inc(agg2_chain, 1)
                    dve.wait_ge(agg2_chain, count(2 * QUADS, nxt, 2 * q + 2))
                    nc.vector.scalar_tensor_tensor(mv2[:, q, 1:2], mv2[:, q, 0:1], mv2[:, q, 0:1], mv2[:, q, 1:2],
                                                   ALU.mult, ALU.add).then_inc(stats2_done, 1)

                def variance2(part):
                    quads = PARTS2[part]
                    dve.wait_ge(mean2_done, count(2, nxt, part + 1))
                    nc.vector.tensor_copy(gs2[:, 0:2, quads], stat2_ps.rearrange("p (q m) -> p m q", m=2)[:, :, quads])\
                      .then_inc(read2_done, 1)
                    dve.wait_ge(read2_done, count(2, nxt, part + 1))
                    nc.vector.tensor_tensor(gs2[:, 5, quads], gs2[:, 0, quads], gs2[:, 0, quads], ALU.mult)\
                      .then_inc(square2, 1)
                    dve.wait_ge(square2, count(2, nxt, part + 1))
                    nc.vector.tensor_tensor(gs2[:, 1, quads], gs2[:, 1, quads], gs2[:, 5, quads], ALU.subtract)\
                      .then_inc(var2_done, 1)

                def scale2(part):
                    quads = PARTS2[part]
                    dve.wait_ge(root2_done, count(2, nxt, part + 1))
                    nc.vector.reciprocal(gs2[:, 3, quads], gs2[:, 2, quads]).then_inc(recip2, 1)
                    dve.wait_ge(recip2, count(2, nxt, part + 1))
                    nc.vector.scalar_tensor_tensor(gs2[:, 4, quads], gs2[:, 0, quads], -1.0, gs2[:, 3, quads],
                                                   ALU.mult, ALU.mult).then_inc(scale2_done, 1)

                def bias_of_h():
                    dve.wait_ge(shift_done, count(1, nxt, 1))
                    nc.vector.tensor_scalar(h_bias[:, :], shift_ps, bn_s[:, 0:1], bn_t[:, 0:1], ALU.mult, ALU.add)\
                      .then_inc(bias_done, 1)

                def differences():
                    dve.wait_ge(h_high, count(1, nxt, 1))
                    nc.vector.tensor_tensor(h_split[:, 1, :], h_sb[:, :], h_split[:, 0, :], ALU.subtract)\
                      .then_inc(h_low, 1)
                    dve.wait_ge(tile_done, count(TILES, nxt, 0))
                    nc.vector.tensor_tensor(dx, h_sb[:, 1:NDX + 1], h_sb[:, 0:NDX], ALU.subtract)\
                      .then_inc(diff_done, 1)
                    nc.vector.tensor_tensor(dy, h_sb[:, PITCH:PITCH + ROWS], h_sb[:, 0:ROWS], ALU.subtract)\
                      .then_inc(diff_done, 1)
                    dve.wait_ge(diff_done, count(3, nxt, 1))
                    nc.vector.tensor_tensor(dxy, dx[:, PITCH:PITCH + ROWS], dx[:, 0:ROWS], ALU.subtract)\
                      .then_inc(diff_done, 1)

                def coordinates():
                    dve.wait_ge(offT_done, count(1, t, 1))
                    nc.vector.tensor_tensor(pos[:, :], offT_ps[:, :], grid_sb[:, :], ALU.add).then_inc(pos_chain, 1)
                    dve.wait_ge(pos_chain, count(8, t, 1))
                    nc.vector.tensor_scalar(pos[:, :], pos[:, :], -1.0, float(HEIGHT), ALU.max, ALU.min)\
                      .then_inc(pos_chain, 1)
                    dve.wait_ge(pos_chain, count(8, t, 2))
                    nc.vector.tensor_copy(posi[:, :], pos[:, :]).then_inc(pos_chain, 1)
                    dve.wait_ge(pos_chain, count(8, t, 3))
                    nc.vector.tensor_copy(posf[:, :], posi[:, :]).then_inc(pos_chain, 1)
                    dve.wait_ge(pos_chain, count(8, t, 4))
                    nc.vector.tensor_tensor(posg[:, :], posf[:, :], pos[:, :], ALU.is_gt).then_inc(pos_chain, 1)
                    dve.wait_ge(pos_chain, count(8, t, 5))
                    nc.vector.tensor_tensor(posf[:, :], posf[:, :], posg[:, :], ALU.subtract).then_inc(pos_chain, 1)
                    dve.wait_ge(pos_chain, count(8, t, 6))
                    nc.vector.tensor_scalar(posf[:, :], posf[:, :], float(HEIGHT - 1), None, ALU.min)\
                      .then_inc(pos_chain, 1)
                    dve.wait_ge(pos_chain, count(8, t, 7))
                    yx = posf[:, :].rearrange("p (a b c) -> p a b c", b=TAPS, c=2)
                    row = posg[:, 0:8 * TAPS].rearrange("p (a b) -> p a b", b=TAPS)
                    nc.vector.scalar_tensor_tensor(row, yx[:, :, :, 0], float(PITCH), yx[:, :, :, 1], ALU.mult,
                                                   ALU.add).then_inc(pos_chain, 1)
                    dve.wait_ge(pos_chain, count(8, t, 8))
                    nc.vector.tensor_scalar(ridx[:, u % 2, :, :], row, float(PITCH + 1), None, ALU.add)
                    nc.vector.tensor_tensor(frac[:, u % 2, :, :, :].rearrange("p a b c -> p (a b c)"), pos[:, :],
                                            posf[:, :], ALU.subtract).then_inc(pos_done, 1)

                for s in range(SLOTS):
                    if a1 and s == VAR1:
                        variance1()
                    if a1 and s == SCALE1:
                        scale1()
                    image, back, c = chunk_at(s, 0, t, tail, b)
                    if image is not None:
                        interpolate(image, (u - back) % 2, c)
                    if s - 1 in SHUFFLE and (a1 if s > NEXT_SHUFFLE else a2):
                        if s > NEXT_SHUFFLE:
                            add_shuffled(new, (u + 2) % XBUFS, *SHUFFLE[s - 1])
                        else:
                            add_shuffled(nxt, (u + 1) % XBUFS, *SHUFFLE[s - 1])
                    if a2 and s in STATS:
                        statistics2(STATS[s])
                    if a2 and s in VAR2:
                        variance2(VAR2.index(s))
                    if a2 and s in SCALE2:
                        scale2(SCALE2.index(s))
                    if a2 and s == SHIFT_SLOT + 1:
                        bias_of_h()
                    for image, back, half, q in outputs_at(s, 5, t, tail, b):
                        add_residual(image, (u - back) % XBUFS, half, q)
                    if a1 and s - 1 in APPLY:
                        low1(APPLY[s - 1])
                    if b and s == COORDINATES:
                        coordinates()
                    if a2 and s == H_SLOT + 1:
                        differences()

            run(dve, step)

        @block.tensor
        def _(pe):
            pe.wait_ge(consts_in, 16 * N_CONSTS)

            def transpose_values(image, c):
                pe.wait_ge(val_done, count(CHUNKS, image, c + 1))
                pe.wait_ge(val_out, count(CHUNKS, image, c - 1))
                for i in range(PER):
                    op = nc.tensor.transpose(valT_ps[c % 2][:, i * CH:(i + 1) * CH],
                                             val[:, c % 2, i * CH:(i + 1) * CH], eye_sb[:, :])
                op.then_inc(valT_done, 1)

            def deform(image, c):
                half, k = divmod(c, TAPS)
                pe.wait_ge(val_out, count(CHUNKS, image, c + 1))
                if k == 0:
                    pe.wait_ge(d_out, count(2, image, half))
                nc.tensor.matmul(def_ps[:, :], wd[:, k * CH:(k + 1) * CH], valT[:, c % 2, :], start=k == 0,
                                 stop=k == TAPS - 1).then_inc(def_done, 1)

            def out_conv(image, half, q):
                if q == 0:
                    pe.wait_ge(d_out, count(2, image, half + 1))
                pe.wait_ge(relu_done, count(2 * QUADS, image, half * QUADS + q))
                nc.tensor.matmul(out_ps[:, :], w2[:, q * 128:(q + 1) * 128], mid[:, :], start=True, stop=True)\
                  .then_inc(out_done, 1)

            def group_conv(image, g, half):
                pe.wait_ge(w_low, 1)
                pe.wait_ge(low1_done, count(2 * QUADS, image, g + 1))
                pe.wait_ge(conv_out, count(2 * GROUPS, image, 2 * g + half - 1))
                if g == 2:
                    pe.wait_ge(h_done, count(2, image - 1, half + 1))
                for k in range(TAPS):
                    ky, kx = divmod(k, 3)
                    op = nc.tensor.matmul(pair_ps[half][:, :], wg[:, g, k, :],
                                          plane(split1[:, g, :], ky + half * HROWS, kx, HROWS),
                                          start=k == 0, stop=k == TAPS - 1)
                op.then_inc(conv_done, 1)

            def shuffle(image, q, half):
                pe.wait_ge(conv_out, count(2 * GROUPS, image, 4 * q + 4))
                pe.wait_ge(mid_done, count(2 * QUADS, image, 2 * q + half))
                if q == 1 and half == 0:
                    pe.wait_ge(tile_out, count(TILES, image - 1, TILES))
                for jj in range(COLS // 2):
                    for e in (0, 1):
                        j = half * (COLS // 2) + jj
                        op = nc.tensor.matmul(
                            shuf_ps[64 * e:64 * e + 64, jj * GIN:(jj + 1) * GIN],
                            conv_sb[:, (2 * q + e) % 3, j:j + COLS * (GIN - 1) + 1:COLS], fold_sb[:, :],
                            start=True, stop=True)
                op.then_inc(shuf_done, 1)

            def offset_conv(image, quarter, third):
                part = quarter // 2
                if quarter == third == 0:
                    pe.wait_ge(bias_done, count(1, image, 1))
                    pe.wait_ge(h_high, count(1, image, 1))
                if quarter == 2 and third == 0:
                    pe.wait_ge(h_low, count(1, image, 1))
                for k in (range(5), range(5, TAPS))[quarter % 2][2 * third:2 * third + 2]:
                    ky, kx = divmod(k, 3)
                    for half in (0, 1):
                        op = nc.tensor.matmul(small_ps[64 * half:64 * half + 64, :], wo[:, k, :],
                                              plane(h_split[:, part, :], ky + half * HROWS, kx, HROWS),
                                              start=part == k == 0, stop=part == 1 and k == TAPS - 1)
                    if part == 1 and k == TAPS - 1:
                        op.then_inc(off_done, 1)

            def step(t, u, tail, b, a2, a1):
                nxt, new = t + 1, t + 2

                def mean1():
                    pe.wait_ge(sums_done, count(2 * QUADS, new, 2 * QUADS))
                    pe.wait_ge(pos_done, count(1, t, 1))
                    nc.tensor.matmul(stat1_ps, blocks_sb[:, :], sums1[:, :, :].rearrange("p a b -> p (a b)"),
                                     start=True, stop=True).then_inc(mean1_done, 1)

                def mean2(part):
                    quads = PARTS2[part]
                    pe.wait_ge(stats2_done, count(QUADS, nxt, quads.stop))
                    if part == 1:
                        pe.wait_ge(read2_done, count(2, nxt, 1))
                    elif a1:
                        pe.wait_ge(read1_done, count(1, new, 1))
                    else:
                        pe.wait_ge(pos_done, count(1, t, 1))
                    nc.tensor.matmul(stat2_ps[:, 2 * quads.start:2 * quads.stop], blocks_sb[:, :],
                                     mv2[:, quads, :].rearrange("p a b -> p (a b)"), start=True, stop=True)\
                      .then_inc(mean2_done, 1)

                def in_conv(q):
                    pe.wait_ge(w1_done, count(QUADS, nxt, q + 1))
                    for half in (0, 1):
                        if q == 0 and a1:
                            pe.wait_ge(conv_out, count(2 * GROUPS, new, 3 + half))
                        elif q == 0:
                            pe.wait_ge(conv_out, count(2 * GROUPS, nxt, 2 * GROUPS - 1 + half))
                        op = nc.tensor.matmul(pair_ps[half][:, :], w1_norm[:, q * CH:(q + 1) * CH],
                                              xs[:, (u + 1) % XBUFS, q, half * HALF:(half + 1) * HALF],
                                              start=q == 0, stop=q == QUADS - 1)
                        if q == QUADS - 1:
                            op.then_inc(in_done, 1)

                def shift_product():
                    pe.wait_ge(scale2_done, count(2, nxt, 2))
                    for q in range(QUADS):
                        op = nc.tensor.matmul(shift_ps, w1[:, q * CH:(q + 1) * CH], gs2[:, 4, q:q + 1], start=q == 0,
                                              stop=q == QUADS - 1)
                    op.then_inc(shift_done, 1)

                def table_tile(m):
                    if m == 0:
                        pe.wait_ge(mid_done, count(2 * QUADS, nxt, 2) if a2 else count(2 * QUADS, t, 2 * QUADS))
                        pe.wait_ge(diff_done, count(3, t, 3))
                    else:
                        pe.wait_ge(tile_out, count(TILES, t, m))
                    r = slice(m * 128, (m + 1) * 128)
                    for i, src in enumerate((h_sb[:, r], dx[:, r], dy[:, r], dxy[:, r])):
                        op = nc.tensor.transpose(shuf_ps[:, i * CH:(i + 1) * CH], src, eye_sb[:, :])
                    op.then_inc(tile_done, 1)

                def transpose_offsets():
                    pe.wait_ge(off_out, count(1, t, 1))
                    by_block = offT_ps.rearrange("p (h i c) -> p i h c", h=2, i=PER)
                    for i in range(PER):
                        op = nc.tensor.matmul(by_block[:, i], offs_sb[:, i * 128:(i + 1) * 128], ofold_sb[:, :],
                                              start=True, stop=True)
                    op.then_inc(offT_done, 1)

                def offsets_and_table(s, place):
                    image = nxt if s == SLOTS - 1 else t
                    if s in OFFSET and (a2 if s == SLOTS - 1 else b) and place < 3:
                        offset_conv(image, OFFSET[s], place)
                    if b and tile_at(s, place) is not None:
                        table_tile(tile_at(s, place))

                for s in range(SLOTS):
                    conv_of = (new if s >= NEXT_CONV else nxt) if (a1 if s >= NEXT_CONV else a2) else None
                    if a2 and s in MEAN2:
                        mean2(MEAN2.index(s))
                    if s < SLOTS - 1:
                        offsets_and_table(s, 0)
                    if conv_of is not None and s in CONV_FIRST:
                        group_conv(conv_of, *CONV_FIRST[s])
                    image, _, c = chunk_at(s, 1, t, tail, b)
                    if image is not None:
                        transpose_values(image, c)
                    if a1 and s == MEAN1:
                        mean1()
                    if a2 and s == SHIFT_SLOT:
                        shift_product()
                    if s < SLOTS - 1:
                        offsets_and_table(s, 1)
                    for q in IN_CONV.get(s, ()) if a2 else ():
                        in_conv(q)
                    if s in SHUFFLE and (a1 if s >= NEXT_SHUFFLE else a2):
                        shuffle(new if s >= NEXT_SHUFFLE else nxt, *SHUFFLE[s])
                    if conv_of is not None and s in CONV_THEN:
                        group_conv(conv_of, *CONV_THEN[s])
                    if s == SLOTS - 1:
                        offsets_and_table(s, 0)
                        offsets_and_table(s, 1)
                    offsets_and_table(s, 2)
                    if b and s == TRANSPOSE_OFFSETS:
                        transpose_offsets()
                    image, _, c = chunk_at(s, 2, t, tail, b)
                    if image is not None:
                        deform(image, c)
                    for image, _, half, q in outputs_at(s, 3, t, tail, b):
                        out_conv(image, half, q)
                    offsets_and_table(s, 3)

            run(pe, step)


def constants():
    import numpy as np

    eye = np.eye(128, dtype=np.float32)
    fold = np.concatenate([np.eye(64, dtype=np.float32)] * 2)
    blocks = np.kron(np.eye(8, dtype=np.float32), np.full((16, 16), 1 / 16, np.float32))
    offset_fold = np.zeros((128, 36), np.float32)
    for half in (0, 1):
        for part in (0, 1):
            for n in range(18):
                offset_fold[64 * half + 18 * part + n, 18 * half + n] = 1
    grid = np.zeros((128, 8, 9, 2), np.float32)
    for p in range(128):
        for i in range(8):
            for k in range(9):
                y, x = divmod(i * 128 + p, 32)
                grid[p, i, k] = (y + k // 3 - 1, x + k % 3 - 1)
    return eye, fold, blocks, offset_fold, grid.reshape(128, -1)


def kernel(x, L0_conv_W, L0_conv_b, L1_conv_conv1_w, L1_conv_conv1_b, L1_conv_bn1_g, L1_conv_bn1_b, L1_conv_bn1_m,
           L1_conv_bn1_v, L1_conv_off_w, L1_conv_off_b, L1_conv_dconv_w, L1_conv_dconv_b, L1_conv_bn2_g,
           L1_conv_bn2_b, L1_conv_bn2_m, L1_conv_bn2_v, L1_conv_conv2_w, L1_conv_conv2_b, L1_conv_bn3_g,
           L1_conv_bn3_b, L1_conv_bn3_m, L1_conv_bn3_v):
    import numpy as np
    import concourse.bacc as bacc
    from concourse.bass_utils import run_bass_kernel_spmd

    def wide(*vectors):
        return np.stack([np.asarray(v).reshape(-1, 128).T for v in vectors], axis=-1)

    eye, fold, blocks, offset_fold, grid = constants()
    bn = np.concatenate([
        wide(L1_conv_bn1_g, L1_conv_bn1_b, L1_conv_bn1_m, L1_conv_bn1_v, L1_conv_conv1_b),
        wide(L1_conv_bn2_g, L1_conv_bn2_b, L1_conv_bn2_m, L1_conv_bn2_v, L1_conv_dconv_b),
        wide(L1_conv_bn3_g, L1_conv_bn3_b, L1_conv_bn3_m, L1_conv_bn3_v, L1_conv_conv2_b)], axis=1)
    arrays = {
        "x": np.asarray(x).reshape(16, 4, 128, 1024),
        "w_group": np.asarray(L0_conv_W).reshape(8, 64, 64, 9).transpose(2, 0, 3, 1).reshape(64, -1),
        "b_group": np.asarray(L0_conv_b).T,
        "w_in": np.asarray(L1_conv_conv1_w).T.reshape(4, 128, 128).transpose(1, 0, 2).reshape(128, -1),
        "w_off": np.asarray(L1_conv_off_w).reshape(18, 128, 9).transpose(1, 2, 0).reshape(128, -1),
        "b_off": np.asarray(L1_conv_off_b).reshape(18, 1),
        "w_def": np.asarray(L1_conv_dconv_w).reshape(128, 128, 9).transpose(1, 2, 0).reshape(128, -1),
        "w_out": np.asarray(L1_conv_conv2_w).T,
        "bn": bn, "eye": eye, "fold": fold, "blocks": blocks, "offset_fold": offset_fold, "grid": grid,
    }
    arrays = {name: np.ascontiguousarray(a) for name, a in arrays.items()}
    nc = bacc.Bacc("TRN2", target_bir_lowering=False, num_devices=1)
    args = [nc.dram_tensor(name, a.shape, mybir.dt.from_np(a.dtype), kind="ExternalInput").ap()
            for name, a in arrays.items()]
    tables = [nc.dram_tensor(f"table{n}", (9 * 128, 512), mybir.dt.float32, kind="Internal").ap() for n in (0, 1)]
    out = nc.dram_tensor("out", (16, 4, 128, 1024), mybir.dt.float32, kind="ExternalOutput").ap()
    build_program(nc, *args, tables, out)
    r = run_bass_kernel_spmd(nc, [arrays], core_ids=[0])
    return r.results[0]["out"].reshape(16, 512, 32, 32)
```
